# Optimizing a Trainium2 kernel written in Bass

```python
import numpy as np
import jax
import jax.numpy as jnp

def _softmax(x, axis=-1):
    return jax.nn.softmax(x, axis=axis)

def _gelu(x):
    return jax.nn.gelu(x, approximate=True)

def _silu(x):
    return jax.nn.silu(x)

def _sigmoid(x):
    return jax.nn.sigmoid(x)

def _layernorm(x, axis=-1, eps=1e-05):
    m = jnp.mean(x, axis=axis, keepdims=True)
    v = jnp.var(x, axis=axis, keepdims=True)
    return (x - m) / jnp.sqrt(v + eps)

def _scatter_add(tgt, idx, src, axis=0):
    return tgt.at[idx].add(src)

def _segment_sum(src, seg, n):
    return jax.ops.segment_sum(src, seg, n)
kernel_name = 'mk_gnn_resnorm_d2_gnn_r8_789b79'

def setup_inputs(seed: int=0):
    np.random.seed(seed)
    _w = jnp.asarray

    def _rec_inputs():
        import jax
        import jax.numpy as jnp
        _gk = jax.random.key(seed)
        x = -0.000202 + 1 * jax.random.normal(jax.random.fold_in(_gk, 1), (12500, 64), jnp.float32)
        _s = jax.random.randint(jax.random.fold_in(_gk, 2), (100000,), 0, 12500, jnp.int32)
        _d = jax.random.randint(jax.random.fold_in(_gk, 3), (100000,), 0, 12500, jnp.int32)
        _loop = jnp.arange(12500, dtype=jnp.int32)
        src = jnp.concatenate([_s, _d, _loop])
        dst = jnp.concatenate([_d, _s, _loop])
        _o = jnp.argsort(dst, stable=True)
        src = src[_o]
        dst = dst[_o]
        edge_attr_64 = -2.25437e-05 + 0.999858 * jax.random.normal(jax.random.fold_in(_gk, 12), (212500, 64), jnp.float32)
        return (x, src, dst, edge_attr_64)
    x, src, dst, edge_attr_64 = _rec_inputs()

    def _L0_gnn_setup():
        import jax, jax.numpy as jnp
        import numpy as np
        N_NODES = 12500
        N_EDGES = 200000
        D_IN = 64
        D_OUT = 64
        key = jax.random.key(seed)
        k1, k2, k3, k4 = jax.random.split(key, 4)
        x = jax.random.normal(k1, (N_NODES, D_IN), dtype=jnp.float32)
        edge_index = jax.random.randint(k2, (2, N_EDGES), 0, N_NODES, dtype=jnp.int64)
        s1 = (6.0 / (D_IN + D_OUT)) ** 0.5
        s2 = (6.0 / (D_OUT + D_OUT)) ** 0.5
        W1 = jax.random.uniform(k3, (D_IN, D_OUT), dtype=jnp.float32, minval=-s1, maxval=s1)
        b1 = jnp.zeros((D_OUT,), dtype=jnp.float32)
        W2 = jax.random.uniform(k4, (D_OUT, D_OUT), dtype=jnp.float32, minval=-s2, maxval=s2)
        b2 = jnp.zeros((D_OUT,), dtype=jnp.float32)
        return {'x': x, 'edge_index': edge_index, 'W1': W1, 'b1': b1, 'W2': W2, 'b2': b2}
    _L0_gnn_all = _L0_gnn_setup()
    _L0_gnn_in = {k: v for k, v in _L0_gnn_all.items() if k in ('W1', 'b1', 'W2', 'b2')}
    del _L0_gnn_all

    def _L1_gnn_setup():
        import jax, jax.numpy as jnp
        import numpy as np
        N_NODES = 12500
        N_EDGES = 125000
        D_NODE = 64
        D_EDGE = 64
        key = jax.random.key(seed)
        ks = jax.random.split(key, 8)
        node_features = jax.random.normal(ks[0], (N_NODES, D_NODE), dtype=jnp.float32)
        edge_features = jax.random.normal(ks[1], (N_EDGES, D_EDGE), dtype=jnp.float32)
        src = jax.random.randint(ks[2], (N_EDGES,), 0, N_NODES)
        tgt = jax.random.randint(ks[3], (N_EDGES,), 0, N_NODES)
        fan_msg = D_NODE + D_EDGE
        W_msg = jax.random.uniform(ks[4], (fan_msg, D_NODE), dtype=jnp.float32, minval=-1.0 / np.sqrt(fan_msg), maxval=1.0 / np.sqrt(fan_msg))
        b_msg = jnp.zeros((D_NODE,), dtype=jnp.float32)
        W_upd = jax.random.uniform(ks[5], (D_NODE, D_NODE), dtype=jnp.float32, minval=-1.0 / np.sqrt(D_NODE), maxval=1.0 / np.sqrt(D_NODE))
        b_upd = jnp.zeros((D_NODE,), dtype=jnp.float32)
        eps = jnp.zeros((1,), dtype=jnp.float32)
        return {'node_features': node_features, 'edge_features': edge_features, 'W_msg': W_msg, 'b_msg': b_msg, 'W_upd': W_upd, 'b_upd': b_upd, 'eps': eps, 'src': src, 'tgt': tgt}
    _L1_gnn_all = _L1_gnn_setup()
    _L1_gnn_in = {k: v for k, v in _L1_gnn_all.items() if k in ('W_msg', 'b_msg', 'W_upd', 'b_upd', 'eps')}
    del _L1_gnn_all
    return {'x': x, 'src': src, 'dst': dst, 'edge_attr_64': edge_attr_64, 'L0_gnn_W1': _L0_gnn_in['W1'], 'L0_gnn_b1': _L0_gnn_in['b1'], 'L0_gnn_W2': _L0_gnn_in['W2'], 'L0_gnn_b2': _L0_gnn_in['b2'], 'L1_gnn_W_msg': _L1_gnn_in['W_msg'], 'L1_gnn_b_msg': _L1_gnn_in['b_msg'], 'L1_gnn_W_upd': _L1_gnn_in['W_upd'], 'L1_gnn_b_upd': _L1_gnn_in['b_upd'], 'L1_gnn_eps': _L1_gnn_in['eps']}

def reference(x, src, dst, edge_attr_64, L0_gnn_W1, L0_gnn_b1, L0_gnn_W2, L0_gnn_b2, L1_gnn_W_msg, L1_gnn_b_msg, L1_gnn_W_upd, L1_gnn_b_upd, L1_gnn_eps):
    import jax
    import jax.numpy as jnp

    def _L0_gnn_ref(x, edge_index, W1, b1, W2, b2):
        import jax, jax.numpy as jnp
        import numpy as np
        N_NODES = 12500
        N_EDGES = 200000
        D_IN = 64
        D_OUT = 64
        src, dst = (edge_index[0], edge_index[1])
        agg = jax.ops.segment_sum(x[src], dst, num_segments=N_NODES)
        h = x + agg
        h = jax.nn.relu(h @ W1 + b1)
        return h @ W2 + b2

    def _L1_gnn_ref(node_features, edge_features, W_msg, b_msg, W_upd, b_upd, eps, src, tgt):
        import jax, jax.numpy as jnp
        import numpy as np
        N_NODES = 12500
        N_EDGES = 125000
        D_NODE = 64
        D_EDGE = 64
        src_feats = node_features[src]
        msg_in = jnp.concatenate([src_feats, edge_features], axis=-1)
        messages = jax.nn.gelu(msg_in @ W_msg + b_msg)
        agg = jax.ops.segment_sum(messages, tgt, num_segments=node_features.shape[0])
        h = (1.0 + eps) * node_features + agg
        out = jax.nn.gelu(h @ W_upd + b_upd)
        return out
    edge_index = jnp.stack([src, dst])
    x = _layernorm(x + _L0_gnn_ref(x, edge_index, L0_gnn_W1, L0_gnn_b1, L0_gnn_W2, L0_gnn_b2), axis=-1)
    x = _layernorm(x + _L1_gnn_ref(x, edge_attr_64, L1_gnn_W_msg, L1_gnn_b_msg, L1_gnn_W_upd, L1_gnn_b_upd, L1_gnn_eps, src, dst), axis=-1)
    return x

_drawn_inputs = setup_inputs


def setup_inputs(seed=0):
    import zlib

    import numpy as np

    out = dict(_drawn_inputs(seed))
    spreads = {'L0_gnn_b1': (0.0, 0.384),
     'L0_gnn_b2': (0.0, 0.27),
     'L1_gnn_b_msg': (0.0, 0.1),
     'L1_gnn_b_upd': (0.0, 0.1)}
    factors = {}
    for name, (base, spread) in spreads.items():
        noise = np.random.default_rng([zlib.crc32(name.encode()), seed]).standard_normal(out[name].shape)
        drawn = base * np.exp(spread * noise) if base else spread * noise
        out[name] = jnp.asarray(drawn.astype(out[name].dtype))
    for name, factor in factors.items():
        out[name] = (out[name] * factor).astype(out[name].dtype)
    return out
```

```python
from contextlib import ExitStack

import concourse.bass as bass
from concourse import mybir

ALU = mybir.AluOpType
ACT = mybir.ActivationFunctionType
AX = mybir.AxisListType
F32 = mybir.dt.float32
I32 = mybir.dt.int32

P = 128
SLOTS = 2
GROUP = 8
CHUNK = 7
LN_EPS = 1e-5


def gnn_kernel(nc, x, src, dst, edge_attr, w1, b1, w2, b2, w_msg, b_msg, w_upd, b_upd, eps, out):
    n_nodes, d = x.shape
    n_edges = src.shape[0]
    tiles = -(-n_edges // P)
    iters = -(-tiles // (SLOTS * GROUP))
    tiles_pad = iters * SLOTS * GROUP
    full_tiles = n_edges // P
    last_edges = n_edges - full_tiles * P
    tile_blocks = -(-tiles_pad // P)
    blocks = -(-n_nodes // P)
    chunks = blocks // CHUNK
    assert blocks % CHUNK == 0 and chunks % 2 == 0 and d == 64
    pairs = chunks // 2
    last_rows = n_nodes - (blocks - 1) * P
    CN = CHUNK * P
    CF = CHUNK * d
    HALF = CN // 2
    GF = GROUP * d
    nodes_pad = blocks * P
    first_node_major = nodes_pad

    msg_table = nc.dram_tensor("msg_table", [first_node_major, d], F32, kind="Internal").ap()

    with ExitStack() as ctx:
        def sb(name, shape, dt=F32):
            return ctx.enter_context(nc.sbuf_tensor(name, shape, dt))

        def sem(name):
            return ctx.enter_context(nc.semaphore(name))

        iota_i = sb("iota_i", [P, P], I32)
        iota_f = sb("iota_f", [P, P])
        ident = sb("ident", [P, P])
        w1_pad = sb("w1_pad", [d, P])
        wupd_pad = sb("wupd_pad", [d, P])
        w2_aug = sb("w2_aug", [d + 1, d])
        wnode_aug = sb("wnode_aug", [d + 1, d])
        wedge_diag = sb("wedge_diag", [P, P])
        b1_col = sb("b1_col", [d, 1])
        bupd_col = sb("bupd_col", [d, 1])
        eps_col = sb("eps_col", [d, 1])
        one_eps = sb("one_eps", [d, 1])
        src_raw = sb("src_raw", [P, tile_blocks * P], I32)
        dst_raw = sb("dst_raw", [P, tile_blocks * P], I32)
        src_f = sb("src_f", [P, tile_blocks * P])
        dst_f = sb("dst_f", [P, tile_blocks * P])
        base_col = sb("base_col", [P, tile_blocks])
        src_idx = sb("src_idx", [P, tile_blocks * P], I32)
        dst_loc = sb("dst_loc", [P, tile_blocks * P])
        base_row = sb("base_row", [1, tile_blocks * P], I32)
        idx_ring = sb("idx_ring", [P, SLOTS, GROUP], I32)
        rows = sb("rows", [P, SLOTS, GF])
        onehot = sb("onehot", [P, SLOTS, GROUP, P])
        ea = sb("ea", [P, SLOTS, GROUP, d])
        eat = sb("eat", [P, SLOTS, GROUP // 2 * P])
        msg = sb("msg", [P, SLOTS, GF])
        acc = sb("acc", [d, nodes_pad + P])
        xc = sb("xc", [P, SLOTS, CF])
        hid = sb("hid", [d + 1, SLOTS, CN])
        v = sb("v", [P, CF])
        sq = sb("sq", [P, CF])
        total = sb("total", [P, CHUNK])
        std = sb("std", [P, CHUNK])
        var1 = sb("var1", [P, blocks])
        std1 = sb("std1", [P, blocks])
        rstd1 = sb("rstd1", [P, blocks])
        ln_eps = sb("ln_eps", [P, 1])
        var = sb("var", [P, CHUNK])
        rstd = sb("rstd", [P, CHUNK])
        x1c = sb("x1c", [P, SLOTS, CF])
        x1t = sb("x1t", [d + 1, SLOTS, CN])
        yc = sb("yc", [P, SLOTS, CF])
        x1 = sb("x1", [P, blocks * d])

        ps = [ctx.enter_context(nc.psum_tensor(f"ps{k}", [P, 2, 512], F32)) for k in range(4)]
        windows = ps[0:2]
        eat_ps = [ps[2][:, 0, :], ps[2][:, 1, :]]
        msg_ps = [ps[3][:, 0, :], ps[3][:, 1, :]]
        init_ps = ps[2:4]
        wide_ps = ps[0:2]
        node_ps = [ps[2][:, 0, 0:CF], ps[2][:, 1, 0:CF]]
        prep_ps = ps

        def flat(t):
            return t[:, :, :].rearrange("p a b -> p (a b)")

        s_src = sem("src_landed")
        s_dst = sem("dst_landed")
        s_w = sem("weights_landed")
        s_wzero = sem("weights_zeroed")
        s_padded = sem("index_pads_set")
        s_iota = sem("iota_made")
        s_ident = sem("ident_made")
        s_idz = sem("ident_zeroed")
        s_eps = sem("one_eps_made")
        s_conv = sem("indices_as_float")
        s_prep_t = sem("prep_transposed")
        src_copied = sem("src_copied")
        dst_copied = sem("dst_copied")
        s_ones = sem("ones_rows_set")
        x_landed = [sem(f"x_landed{h}") for h in range(SLOTS)]
        init_t = sem("init_transposed")
        init_done = sem("init_copied")

        class Layer:
            pass

        def layer(n):
            s = Layer()
            s.idx_ready = [sem(f"l{n}_idx_ready{h}") for h in range(SLOTS)]
            s.gathered = [sem(f"l{n}_gathered{h}") for h in range(SLOTS)]
            s.onehot_ready = [sem(f"l{n}_onehot_ready{h}") for h in range(SLOTS)]
            s.windows_done = [sem(f"l{n}_windows_done{h}") for h in range(SLOTS)]
            s.acc_added = sem(f"l{n}_acc_added")
            return s

        L = [layer(0), layer(1)]
        ea_landed = [sem(f"ea_landed{h}") for h in range(SLOTS)]
        ea_transposed = [sem(f"ea_transposed{h}") for h in range(SLOTS)]
        eat_ready = [sem(f"eat_ready{h}") for h in range(SLOTS)]
        msg_summed = [sem(f"msg_summed{h}") for h in range(SLOTS)]
        msg_ready = [sem(f"msg_ready{h}") for h in range(SLOTS)]

        def node(n):
            s = Layer()
            s.x_landed = [sem(f"n{n}_x_landed{h}") for h in range(SLOTS)]
            s.up_done = [sem(f"n{n}_up_done{h}") for h in range(SLOTS)]
            s.hid_ready = [sem(f"n{n}_hid_ready{h}") for h in range(SLOTS)]
            s.out_done = [sem(f"n{n}_out_done{h}") for h in range(SLOTS)]
            s.ln_step = sem(f"n{n}_ln_step")
            s.stored = [sem(f"n{n}_stored{h}") for h in range(SLOTS)]
            return s

        N0, N1 = node(0), node(1)
        x1_transposed = [sem(f"x1_transposed{h}") for h in range(SLOTS)]
        x1t_ready = [sem(f"x1t_ready{h}") for h in range(SLOTS)]
        x1_kept = [sem(f"x1_kept{h}") for h in range(SLOTS)]
        acc_set = [sem(f"acc_set{h}") for h in range(SLOTS)]
        y_summed = [sem(f"y_summed{h}") for h in range(SLOTS)]
        y_ready = [sem(f"y_ready{h}") for h in range(SLOTS)]
        std_ready = sem("std_ready")
        s_rstd1 = sem("rstd1_made")
        s_lneps = sem("ln_eps_set")
        out_ready = sem("out_ready")
        out_stored = sem("out_stored")
        STEPS0, STEPS1 = 7, 5
        W_LOADS = 11

        def tile_at(i, h):
            return i * (SLOTS * GROUP) + h * GROUP

        def over_groups(eng, body):
            for h in range(SLOTS):
                body(0, h, True)
            with eng.Fori(1, iters) as i:
                for h in range(SLOTS):
                    body(i, h, False)

        def over_chunks(eng, lead, follow):
            def step(i, last=False):
                lead(2 * i + 1, 1, i)
                follow(2 * i, 0, i)
                if not last:
                    lead(2 * i + 2, 0, i + 1)
                follow(2 * i + 1, 1, i)
            lead(0, 0, 0)
            step(0)
            with eng.Fori(1, pairs - 1) as i:
                step(i)
            step(pairs - 1, last=True)

        def alone(eng):
            eng.nop(nofuse=True)

        def used(u):
            return not (isinstance(u, int) and u == 0)

        block = ctx.enter_context(nc.Block())

        @block.sync
        def _(sp):
            whole = full_tiles // P
            rest = full_tiles - whole * P
            sp.wait_ge(s_padded, 2)
            for raw, ap, s in ((src_raw, src, s_src), (dst_raw, dst, s_dst)):
                sp.dma_start(raw[:, 0:whole * P].rearrange("p (k e) -> p k e", e=P),
                             ap[0:whole * P * P].rearrange("(k p e) -> p k e", p=P, e=P)).then_inc(s, 16)
                sp.dma_start(raw[0:rest, whole * P:(whole + 1) * P],
                             ap[whole * P * P:full_tiles * P].rearrange("(p e) -> p e", e=P)).then_inc(s, 16)
                sp.dma_start(raw[rest:rest + 1, whole * P:whole * P + last_edges],
                             ap[full_tiles * P:n_edges].rearrange("(p e) -> p e", p=1)).then_inc(s, 16)
            sp.wait_ge(s_wzero, 3)
            sp.dma_start(w1_pad[:, 0:d], w1).then_inc(s_w, 16)
            sp.dma_start(wupd_pad[:, 0:d], w_upd).then_inc(s_w, 16)
            sp.dma_start(w2_aug[0:d, :], w2).then_inc(s_w, 16)
            sp.dma_start(w2_aug[d:d + 1, :], b2.rearrange("(a f) -> a f", a=1)).then_inc(s_w, 16)
            sp.dma_start(wnode_aug[0:d, :], w_msg[0:d, :]).then_inc(s_w, 16)
            sp.dma_start(wnode_aug[d:d + 1, :], b_msg.rearrange("(a f) -> a f", a=1)).then_inc(s_w, 16)
            sp.dma_start(wedge_diag[0:d, 0:d], w_msg[d:2 * d, :]).then_inc(s_w, 16)
            sp.dma_start(wedge_diag[d:2 * d, d:2 * d], w_msg[d:2 * d, :]).then_inc(s_w, 16)
            sp.dma_start(b1_col[:, :], b1.rearrange("(f a) -> f a", a=1)).then_inc(s_w, 16)
            sp.dma_start(bupd_col[:, :], b_upd.rearrange("(f a) -> f a", a=1)).then_inc(s_w, 16)
            sp.dma_start(eps_col[:, :], eps.rearrange("(f a) -> f a", a=1).to_broadcast([d, 1])
                         ).then_inc(s_w, 16)

            def load_x(c, h, s, last=False):
                nb = CHUNK - 1 if last else CHUNK
                sp.dma_start(xc[:, h, 0:nb * d].rearrange("p (b f) -> p b f", f=d),
                             x[bass.ds(c * CN, nb * P), :].rearrange("(b p) f -> p b f", p=P)
                             ).then_inc(s[h], 16)
                if last:
                    sp.dma_start(xc[0:last_rows, h, nb * d:CF], x[n_nodes - last_rows:n_nodes, :]
                                 ).then_inc(s[h], 16)

            for c in range(2):
                load_x(c, c, x_landed)
            with sp.Fori(1, pairs - 1) as i:
                for h in range(SLOTS):
                    sp.wait_ge(init_t, 2 * i + h - 1)
                    load_x(2 * i + h, h, x_landed)
            for h in range(SLOTS):
                sp.wait_ge(init_t, chunks - 3 + h)
                load_x(chunks - 2 + h, h, x_landed, last=h == 1)

            def load_lead(c, h, u):
                if used(u):
                    sp.wait_ge(N0.ln_step, STEPS0 * (c - 2) + 1)
                else:
                    sp.wait_ge(init_t, chunks)
                load_x(c, h, N0.x_landed, last=isinstance(c, int) and c == chunks - 1)

            def store_y(c, h, u):
                sp.wait_ge(y_ready[h], u + 1)
                sp.dma_start(msg_table[bass.ds(c * CN, CN), :].rearrange("(b p) f -> p b f", p=P),
                             yc[:, h, :].rearrange("p (b f) -> p b f", f=d)).then_inc(N0.stored[h], 16)

            over_chunks(sp, load_lead, store_y)

            def load_ea(i, h, first, n=GROUP):
                if not first:
                    sp.wait_ge(ea_transposed[h], i)
                sp.dma_start(ea[:, h, 0:n, :],
                             edge_attr[bass.ds(tile_at(i, h) * P, n * P), :].rearrange("(t p) f -> p t f", p=P)
                             ).then_inc(ea_landed[h], 16)

            for h in range(SLOTS):
                load_ea(0, h, True)
            with sp.Fori(1, iters - 1) as i:
                for h in range(SLOTS):
                    load_ea(i, h, False)
            i = iters - 1
            load_ea(i, 0, False)
            n = full_tiles - tile_at(i, 1)
            load_ea(i, 1, False, n)
            sp.dma_start(ea[0:last_edges, 1, n, :], edge_attr[full_tiles * P:n_edges, :]
                         ).then_inc(ea_landed[1], 16)

            for c in range(chunks):
                last = c == chunks - 1
                nb = CHUNK - 1 if last else CHUNK
                sp.wait_ge(out_ready, c + 1)
                sp.dma_start(out[c * CN:c * CN + nb * P, :].rearrange("(b p) f -> p b f", p=P),
                             x1[:, c * CF:c * CF + nb * d].rearrange("p (b f) -> p b f", f=d)).then_inc(out_stored, 16)
            sp.dma_start(out[n_nodes - last_rows:n_nodes, :], x1[0:last_rows, (blocks - 1) * d:]
                         ).then_inc(out_stored, 16)
            sp.wait_ge(out_stored, 16 * (chunks + 1))

        @block.gpsimd
        def _(pool):
            nc.gpsimd.iota(iota_i[:, :], pattern=[[1, P]], base=0, channel_multiplier=0).then_inc(s_iota, 1)
            nc.gpsimd.memset(ident[:, :], 0.0).then_inc(s_idz, 1)
            pool.wait_ge(s_idz, 1)
            nc.gpsimd.affine_select(out=ident[:, :], in_=ident[:, :], compare_op=ALU.not_equal, fill=1.0,
                                    base=0, pattern=[[-1, P]], channel_multiplier=1).then_inc(s_ident, 1)

            def gather_from(table, s, rows_used):
                def gather(i, h, first):
                    if not first:
                        pool.wait_ge(rows_used[h], i)
                    pool.wait_ge(s.idx_ready[h], i + 1)
                    alone(pool)
                    for k in range(GROUP):
                        pool.indirect_dma_start(
                            out=rows[:, h, k * d:(k + 1) * d], out_offset=None, in_=table,
                            in_offset=bass.IndirectOffsetOnAxis(ap=idx_ring[:, h, k:k + 1], axis=0),
                        ).then_inc(s.gathered[h], 16)
                return gather

            over_groups(pool, gather_from(x[:, :], L[0], L[0].windows_done))

            def keep_x1(c, h, u):
                pool.wait_ge(N0.ln_step, STEPS0 * c + STEPS0)
                nc.gpsimd.tensor_copy(x1[:, bass.ds(c * CF, CF)], x1c[:, h, :]).then_inc(x1_kept[h], 1)

            with pool.Fori(0, pairs) as i:
                for h in range(SLOTS):
                    keep_x1(2 * i + h, h, i)
            for h in range(SLOTS):
                pool.wait_ge(N0.stored[h], 16 * pairs)
            over_groups(pool, gather_from(msg_table[:, :], L[1], msg_summed))

        @block.scalar
        def _(act):
            for q in range(0, tile_blocks, 4):
                nb = min(4, tile_blocks - q)
                act.wait_ge(s_prep_t, q // 4 + 1)
                nc.scalar.copy(src_idx[:, q * P:(q + nb) * P], ps[q // 4 % 2][:, 0, 0:nb * P]).then_inc(src_copied, 1)

            def init_copy(c, h):
                act.wait_ge(init_t, c + 1)
                nc.scalar.copy(acc[:, bass.ds(c * CN, CN)], flat(init_ps[h])[0:d, 0:CN]).then_inc(init_done, 1)

            def copy_idx(s, i, h, first):
                if not first:
                    act.wait_ge(s.gathered[h], 16 * GROUP * i)
                nc.scalar.copy(idx_ring[:, h, :], src_idx[:, bass.ds(tile_at(i, h), GROUP)]
                               ).then_inc(s.idx_ready[h], 1)

            act.wait_ge(src_copied, -(-tile_blocks // 4))
            for h in range(SLOTS):
                copy_idx(L[0], 0, h, True)
            with act.Fori(0, pairs) as i:
                for h in range(SLOTS):
                    init_copy(2 * i + h, h)
            with act.Fori(1, iters) as i:
                for h in range(SLOTS):
                    copy_idx(L[0], i, h, False)

            act.wait_ge(s_w, 16 * W_LOADS)
            act.wait_ge(s_ones, 2)
            act.wait_ge(s_eps, 1)
            act.wait_ge(s_lneps, 1)

            def hidden(s, func, bias):
                def lead(c, h, u):
                    act.wait_ge(s.up_done[h], u + 1)
                    if used(u):
                        act.wait_ge(s.out_done[h], u)
                    nc.scalar.activation(hid[0:d, h, :].rearrange("p (a b) -> p a b", a=2),
                                         wide_ps[h][0:d, :, 0:HALF], func, bias=bias).then_inc(s.hid_ready[h], 1)
                return lead

            def after_norm(c, h, u):
                act.wait_ge(N0.ln_step, STEPS0 * c + 5)
                nc.scalar.activation(std[:, :], var[:, :], ACT.Sqrt, bias=ln_eps[:, 0:1], scale=1.0 / d
                                     ).then_inc(std_ready, 1)
                act.wait_ge(x1_transposed[h], u + 1)
                if used(u):
                    act.wait_ge(y_summed[h], u)
                nc.scalar.copy(x1t[0:d, h, :], flat(wide_ps[h])[0:d, 0:CN]).then_inc(x1t_ready[h], 1)
                nc.scalar.activation(acc[:, bass.ds(c * CN, CN)], flat(wide_ps[h])[0:d, 0:CN],
                                     ACT.Copy, scale=one_eps[:, 0:1]).then_inc(acc_set[h], 1)
                act.wait_ge(y_summed[h], u + 1)
                if used(u):
                    act.wait_ge(N0.stored[h], 16 * u)
                nc.scalar.copy(yc[:, h, :], node_ps[h]).then_inc(y_ready[h], 1)

            over_chunks(act, hidden(N0, ACT.Relu, b1_col[:, 0:1]), after_norm)

            def edge(i, h, first):
                copy_idx(L[1], i, h, first)
                act.wait_ge(ea_transposed[h], i + 1)
                if not first:
                    act.wait_ge(msg_summed[h], i)
                nc.scalar.copy(eat[:, h, :], eat_ps[h]).then_inc(eat_ready[h], 1)
                act.wait_ge(msg_summed[h], i + 1)
                if not first:
                    act.wait_ge(L[1].windows_done[h], i)
                nc.scalar.activation(msg[:, h, :], msg_ps[h], ACT.Gelu_apprx_tanh).then_inc(msg_ready[h], 1)

            over_groups(act, edge)

            def nothing(c, h, u):
                pass

            over_chunks(act, hidden(N1, ACT.Gelu_apprx_tanh, bupd_col[:, 0:1]), nothing)
            act.wait_ge(N1.ln_step, STEPS1 * chunks)
            nc.scalar.activation(std1[:, :], var1[:, :], ACT.Sqrt, bias=ln_eps[:, 0:1], scale=1.0 / d
                                 ).then_inc(std_ready, 1)

        @block.vector
        def _(dve):
            short = (tile_blocks - 1) * P
            nc.vector.memset(src_raw[:, short:], 0).then_inc(s_padded, 1)
            nc.vector.memset(dst_raw[:, short:], -1).then_inc(s_padded, 1)
            nc.vector.memset(w1_pad[:, :], 0.0).then_inc(s_wzero, 1)
            nc.vector.memset(wupd_pad[:, :], 0.0).then_inc(s_wzero, 1)
            nc.vector.memset(wedge_diag[:, :], 0.0).then_inc(s_wzero, 1)
            nc.vector.memset(hid[d:d + 1, :, :], 1.0).then_inc(s_ones, 1)
            nc.vector.memset(x1t[d:d + 1, :, :], 1.0).then_inc(s_ones, 1)
            nc.vector.memset(ln_eps[:, :], LN_EPS).then_inc(s_lneps, 1)
            nc.vector.memset(acc[:, nodes_pad:], 0.0)
            dve.wait_ge(s_src, 48)
            nc.vector.tensor_copy(src_f[:, :], src_raw[:, :]).then_inc(s_conv, 1)
            dve.wait_ge(s_dst, 48)
            nc.vector.tensor_copy(dst_f[:, :], dst_raw[:, :]).then_inc(s_conv, 1)
            dve.wait_ge(s_conv, 2)
            d3 = dst_f[:, :].rearrange("p (k e) -> p k e", e=P)
            nc.vector.tensor_scalar(base_col[:, :], d3[:, :, 0], 0.0, None, ALU.max).then_inc(s_conv, 1)
            dve.wait_ge(s_conv, 3)
            for k in range(tile_blocks):
                nc.vector.tensor_scalar(d3[:, k, :], d3[:, k, :], base_col[:, k:k + 1], None, ALU.subtract
                                        ).then_inc(s_conv, 1)
            dve.wait_ge(s_iota, 1)
            nc.vector.tensor_copy(iota_f[:, :], iota_i[:, :]).then_inc(s_conv, 1)
            dve.wait_ge(s_w, 16 * W_LOADS)
            nc.vector.tensor_scalar(one_eps[:, :], eps_col[:, :], 1.0, None, ALU.add).then_inc(s_eps, 1)
            groups = -(-tile_blocks // 4)
            for q in range(0, tile_blocks, 4):
                nb = min(4, tile_blocks - q)
                dve.wait_ge(s_prep_t, q // 4 + 1)
                nc.vector.tensor_copy(dst_loc[:, q * P:(q + nb) * P], ps[q // 4 % 2][:, 1, 0:nb * P])
                nc.vector.tensor_copy(base_row[:, q * P:(q + nb) * P], ps[2 + q // 4 % 2][0:1, 0, 0:nb * P]
                                      ).then_inc(dst_copied, 1)
            dve.wait_ge(dst_copied, groups)

            def edges(s, ready):
                def body(i, h, first):
                    t = tile_at(i, h)
                    if not first:
                        dve.wait_ge(s.windows_done[h], i)
                    nc.vector.tensor_tensor(
                        onehot[:, h, :, :],
                        iota_f[:, :].rearrange("p (a n) -> p a n", a=1).to_broadcast([P, GROUP, P]),
                        dst_loc[:, bass.ds(t, GROUP)].rearrange("p (g a) -> p g a", a=1).to_broadcast([P, GROUP, P]),
                        ALU.is_equal).then_inc(s.onehot_ready[h], 1)
                    bases = [dve.value_load(base_row[0:1, bass.ds(t + k, 1)], min_val=0, max_val=n_nodes - 1)
                             for k in range(GROUP)]
                    dve.wait_ge(s.windows_done[h], i + 1)
                    for k in range(GROUP):
                        if not (first and h == 0 and k == 0):
                            dve.wait_ge(s.acc_added, t + k)
                        else:
                            ready()
                        window = acc[:, bass.ds(bases[k], P)]
                        nc.vector.tensor_tensor(window, window, flat(windows[h])[0:d, k * P:(k + 1) * P],
                                                ALU.add).then_inc(s.acc_added, 1)
                return body

            over_groups(dve, edges(L[0], lambda: dve.wait_ge(init_done, chunks)))

            def three(t):
                return t.rearrange("p (b f) -> p b f", f=d)

            def over_f(t):
                return t.rearrange("p (b a) -> p b a", a=1).to_broadcast([P, CHUNK, d])

            def center(s, steps, c, vc, total, squares, psum, resid):
                def step(k):
                    dve.wait_ge(s.ln_step, steps * c + k)
                    if k == 1:
                        alone(dve)
                if used(c):
                    step(0)
                nc.vector.tensor_tensor(vc, psum, resid, ALU.add).then_inc(s.ln_step, 1)
                step(1)
                nc.vector.tensor_reduce(total[:, :], three(vc), AX.X, ALU.add).then_inc(s.ln_step, 1)
                step(2)
                nc.vector.scalar_tensor_tensor(out=three(vc), in0=over_f(total[:, :]), scalar=-1.0 / d,
                                               in1=three(vc), op0=ALU.mult, op1=ALU.add).then_inc(s.ln_step, 1)
                step(3)
                nc.vector.tensor_tensor(sq[:, :], vc, vc, ALU.mult).then_inc(s.ln_step, 1)
                step(4)
                nc.vector.tensor_reduce(squares, three(sq[:, :]), AX.X, ALU.add).then_inc(s.ln_step, 1)

            def norm0(c, h, u):
                last = isinstance(c, int) and c == chunks - 1
                dve.wait_ge(N0.out_done[h], u + 1)
                dve.wait_ge(N0.x_landed[h], 16 * u + (32 if last else 16))
                center(N0, STEPS0, c, v[:, :], total, var[:, :], node_ps[h], xc[:, h, :])
                dve.wait_ge(std_ready, c + 1)
                nc.vector.reciprocal(rstd[:, :], std[:, :]).then_inc(N0.ln_step, 1)
                dve.wait_ge(N0.ln_step, STEPS0 * c + 6)
                if used(u):
                    dve.wait_ge(x1_transposed[h], u)
                    dve.wait_ge(x1_kept[h], u)
                nc.vector.tensor_tensor(three(x1c[:, h, :]), three(v[:, :]), over_f(rstd[:, :]), ALU.mult
                                        ).then_inc(N0.ln_step, 1)

            def over_slots(body):
                for h in range(SLOTS):
                    body(h, h, 0)
                with dve.Fori(1, pairs - 1) as i:
                    for h in range(SLOTS):
                        body(2 * i + h, h, i)
                for h in range(SLOTS):
                    body(chunks - 2 + h, h, pairs - 1)

            over_slots(norm0)

            def ready():
                for h in range(SLOTS):
                    dve.wait_ge(x1_kept[h], pairs)
                    dve.wait_ge(acc_set[h], pairs)

            over_groups(dve, edges(L[1], ready))

            def norm1(c, h, u):
                dve.wait_ge(N1.out_done[h], u + 1)
                x1_chunk = x1[:, bass.ds(c * CF, CF)]
                center(N1, STEPS1, c, x1_chunk, total, var1[:, bass.ds(c * CHUNK, CHUNK)], node_ps[h], x1_chunk)

            over_slots(norm1)
            dve.wait_ge(std_ready, chunks + 1)
            nc.vector.reciprocal(rstd1[:, :], std1[:, :]).then_inc(s_rstd1, 1)
            dve.wait_ge(s_rstd1, 1)
            for c in range(chunks):
                x1_chunk = three(x1[:, c * CF:(c + 1) * CF])
                nc.vector.tensor_tensor(x1_chunk, x1_chunk, over_f(rstd1[:, c * CHUNK:(c + 1) * CHUNK]), ALU.mult
                                        ).then_inc(out_ready, 1)

        @block.tensor
        def _(pe):
            pe.wait_ge(s_ident, 1)
            pe.wait_ge(s_conv, 3 + tile_blocks)
            for q in range(0, tile_blocks, 4):
                g = q // 4
                if g >= 2:
                    pe.wait_ge(src_copied, g - 1)
                    pe.wait_ge(dst_copied, g - 1)
                for k in range(q, min(q + 4, tile_blocks)):
                    c0 = (k - q) * P
                    nc.tensor.transpose(ps[g % 2][:, 0, c0:c0 + P], src_f[:, k * P:(k + 1) * P], ident[:, :])
                    nc.tensor.transpose(ps[g % 2][:, 1, c0:c0 + P], dst_f[:, k * P:(k + 1) * P], ident[:, :])
                    mm = nc.tensor.matmul(ps[2 + g % 2][0:1, 0, c0:c0 + P], base_col[:, k:k + 1], ident[:, :],
                                          start=True, stop=True)
                mm.then_inc(s_prep_t, 1)
            pe.wait_ge(src_copied, -(-tile_blocks // 4))
            pe.wait_ge(dst_copied, -(-tile_blocks // 4))

            def init(c, h, u, last=False):
                pe.wait_ge(x_landed[h], 16 * u + (32 if last else 16))
                if used(u):
                    pe.wait_ge(init_done, c - 1)
                alone(pe)
                for b in range(CHUNK):
                    mm = nc.tensor.transpose(flat(init_ps[h])[0:d, b * P:(b + 1) * P],
                                             xc[:, h, b * d:(b + 1) * d], ident[:, :])
                mm.then_inc(init_t, 1)

            for h in range(SLOTS):
                init(h, h, 0)
            with pe.Fori(1, pairs - 1) as i:
                for h in range(SLOTS):
                    init(2 * i + h, h, i)
            for h in range(SLOTS):
                init(chunks - 2 + h, h, pairs - 1, last=h == 1)

            def sum_tiles(s, rhs, i, h, first, done=()):
                pe.wait_ge(s.onehot_ready[h], i + 1)
                if not first:
                    pe.wait_ge(s.acc_added, tile_at(i, h) - GROUP)
                for k in range(GROUP):
                    mm = nc.tensor.matmul(flat(windows[h])[0:d, k * P:(k + 1) * P],
                                          rhs[:, h, k * d:(k + 1) * d], onehot[:, h, k, :],
                                          start=True, stop=True)
                mm.then_inc(s.windows_done[h], 1)

            def edge0(i, h, first):
                pe.wait_ge(L[0].gathered[h], 16 * GROUP * (i + 1))
                sum_tiles(L[0], rows, i, h, first)

            over_groups(pe, edge0)

            pe.wait_ge(s_w, 16 * W_LOADS)
            pe.wait_ge(L[0].acc_added, tiles_pad)

            def up(s, w, c, h, u):
                for a in range(2):
                    mm = nc.tensor.matmul(wide_ps[h][:, a, 0:HALF], w[:, :],
                                          acc[:, bass.ds(c * CN + a * HALF, HALF)], start=True, stop=True)
                mm.then_inc(s.up_done[h], 1)

            def lead0(c, h, u):
                if used(u):
                    pe.wait_ge(acc_set[h], u)
                    pe.wait_ge(y_ready[h], u)
                up(N0, w1_pad, c, h, u)
                pe.wait_ge(N0.hid_ready[h], u + 1)
                for b in range(CHUNK):
                    mm = nc.tensor.matmul(node_ps[h][:, b * d:(b + 1) * d], hid[:, h, b * P:(b + 1) * P],
                                          w2_aug[:, :], start=True, stop=True)
                mm.then_inc(N0.out_done[h], 1)

            def follow0(c, h, u):
                pe.wait_ge(N0.ln_step, STEPS0 * c + STEPS0)
                alone(pe)
                for b in range(CHUNK):
                    mm = nc.tensor.transpose(flat(wide_ps[h])[0:d, b * P:(b + 1) * P],
                                             x1c[:, h, b * d:(b + 1) * d], ident[:, :])
                mm.then_inc(x1_transposed[h], 1)
                pe.wait_ge(x1t_ready[h], u + 1)
                for b in range(CHUNK):
                    mm = nc.tensor.matmul(node_ps[h][:, b * d:(b + 1) * d], x1t[:, h, b * P:(b + 1) * P],
                                          wnode_aug[:, :], start=True, stop=True)
                mm.then_inc(y_summed[h], 1)

            over_chunks(pe, lead0, follow0)
            for h in range(SLOTS):
                pe.wait_ge(y_ready[h], pairs)
                pe.wait_ge(acc_set[h], pairs)

            def edge1(i, h, first):
                pe.wait_ge(ea_landed[h], 16 * (i + 1) + (16 if isinstance(i, int) and i == iters - 1 and h == 1 else 0))
                if not first:
                    pe.wait_ge(eat_ready[h], i)
                alone(pe)
                for k in range(GROUP // 2):
                    mm = nc.tensor.transpose(eat_ps[h][:, k * P:(k + 1) * P],
                                             ea[:, h, 2 * k:2 * k + 2, :].rearrange("p a f -> p (a f)"), ident[:, :])
                mm.then_inc(ea_transposed[h], 1)
                pe.wait_ge(L[1].gathered[h], 16 * GROUP * (i + 1))
                if not first:
                    pe.wait_ge(msg_ready[h], i)
                nc.tensor.matmul(msg_ps[h], ident[:, :], rows[:, h, :], start=True, stop=True)
                pe.wait_ge(eat_ready[h], i + 1)
                for k in range(GROUP // 2):
                    mm = nc.tensor.matmul(msg_ps[h][:, k * P:(k + 1) * P], eat[:, h, k * P:(k + 1) * P],
                                          wedge_diag[:, :], start=False, stop=True,
                                          skip_group_check=True)
                mm.then_inc(msg_summed[h], 1)
                pe.wait_ge(msg_ready[h], i + 1)
                sum_tiles(L[1], msg, i, h, first)

            for h in range(SLOTS):
                edge1(0, h, True)
            with pe.Fori(1, iters - 1) as i:
                for h in range(SLOTS):
                    edge1(i, h, False)
            for h in range(SLOTS):
                edge1(iters - 1, h, False)

            pe.wait_ge(L[1].acc_added, tiles_pad)

            def lead1(c, h, u):
                if used(u):
                    pe.wait_ge(N1.ln_step, STEPS1 * (c - 2) + 1)
                up(N1, wupd_pad, c, h, u)
                pe.wait_ge(N1.hid_ready[h], u + 1)
                alone(pe)
                for b in range(CHUNK):
                    mm = nc.tensor.transpose(node_ps[h][:, b * d:(b + 1) * d], hid[0:d, h, b * P:(b + 1) * P],
                                             ident[0:d, 0:d])
                mm.then_inc(N1.out_done[h], 1)

            over_chunks(pe, lead1, lambda c, h, u: None)


_INS = ["x", "src", "dst", "edge_attr_64", "L0_gnn_W1", "L0_gnn_b1", "L0_gnn_W2", "L0_gnn_b2",
        "L1_gnn_W_msg", "L1_gnn_b_msg", "L1_gnn_W_upd", "L1_gnn_b_upd", "L1_gnn_eps"]


def kernel(**inputs):
    import numpy as _np
    import concourse.bacc as _bacc
    from concourse import mybir as _mybir
    from concourse.bass_utils import run_bass_kernel_spmd as _run

    nc = _bacc.Bacc("TRN2", target_bir_lowering=False, num_devices=1)
    arrays, args = {}, []
    for name in _INS:
        a = _np.ascontiguousarray(inputs[name])
        arrays[f"in_{name}"] = a
        args.append(nc.dram_tensor(f"in_{name}", a.shape, _mybir.dt.from_np(a.dtype), kind="ExternalInput").ap())
    shape = inputs["x"].shape
    args.append(nc.dram_tensor("out_0", shape, F32, kind="ExternalOutput").ap())
    gnn_kernel(nc, *args)
    r = _run(nc, [arrays], core_ids=[0])
    return r.results[0]["out_0"]
```

```python
from contextlib import ExitStack

import concourse.bass as bass
from concourse import mybir

ALU = mybir.AluOpType
ACT = mybir.ActivationFunctionType
AX = mybir.AxisListType
F32 = mybir.dt.float32
I32 = mybir.dt.int32

P = 128
BANK = 512
SLOTS = 2
GROUP = 8
WINDOW = 96
CHUNK = 14
LN_EPS = 1e-5


def gnn_kernel(nc, x, src, dst, edge_attr, w1, b1, w2, b2, w_msg, b_msg, w_upd, b_upd, eps, out):
    n_nodes, d = x.shape
    n_edges = src.shape[0]
    tiles = -(-n_edges // P)
    iters = -(-tiles // (SLOTS * GROUP))
    tiles_pad = iters * SLOTS * GROUP
    n_groups = iters * SLOTS
    full_tiles = n_edges // P
    last_edges = n_edges - full_tiles * P
    TB = -(-tiles_pad // P)
    blocks = n_nodes // P + 1
    chunks = blocks // CHUNK
    pairs = CHUNK // 2
    last_rows = n_nodes - (blocks - 1) * P
    CN = CHUNK * P
    CF = CHUNK * d
    HALF = CF // 2
    GF = GROUP * d
    SWEEPS = -(-n_nodes // BANK)
    assert blocks == chunks * CHUNK and chunks == 7 and 2 * d == P and TB * P == tiles_pad and TB == 13

    msg_table = nc.dram_tensor("msg_table", [blocks * P, d], F32, kind="Internal").ap()

    with ExitStack() as ctx:
        def sb(name, shape, dt=F32):
            return ctx.enter_context(nc.sbuf_tensor(name, shape, dt))

        def sem(name):
            return ctx.enter_context(nc.semaphore(name))

        def sems(name):
            return [sem(f"{name}{h}") for h in range(SLOTS)]

        iota_i = sb("iota_i", [P, BANK], I32)
        iota_f = sb("iota_f", [P, BANK])
        ident = sb("ident", [P, P])
        spread = sb("spread", [P, P])
        w1_diag = sb("w1_diag", [P, P])
        w2_diag = sb("w2_diag", [P, P])
        wnode_diag = sb("wnode_diag", [P, P])
        wedge_diag = sb("wedge_diag", [P, P])
        wupd_diag = sb("wupd_diag", [P, P])
        b1_col = sb("b1_col", [P, 1])
        bupd_col = sb("bupd_col", [P, 1])
        b2_rows = sb("b2_rows", [P, d])
        bmsg_rows = sb("bmsg_rows", [P, d])
        one_eps = sb("one_eps", [P, 1])
        ln_eps = sb("ln_eps", [P, 1])
        src_raw = sb("src_raw", [P, TB * P], I32)
        dst_raw = sb("dst_raw", [P, TB * P], I32)
        src_f = sb("src_f", [P, TB * P])
        dst_f = sb("dst_f", [P, TB * P])
        loc_f = src_raw[:, :].bitcast(F32)
        left_f = dst_raw[:, :].bitcast(F32)
        left_max = sb("left_max", [P, 1])
        base_col = sb("base_col", [P, TB])
        src_idx = sb("src_idx", [P, TB * P], I32)
        dst_loc = sb("dst_loc", [P, TB * P])
        dst_left = sb("dst_left", [P, TB * P])
        base_row = sb("base_row", [1, n_groups], I32)
        left_flag = sb("left_flag", [1, 1], I32)
        idx_ring = sb("idx_ring", [P, SLOTS, GROUP], I32)
        rows = sb("rows", [P, SLOTS, GF])
        onehot = sb("onehot", [P, SLOTS, GROUP, WINDOW])
        ea = sb("ea", [P, SLOTS, GROUP, d])
        eat = sb("eat", [P, SLOTS, GROUP // 2 * P])
        pre = sb("pre", [P, SLOTS, GF])
        msg = sb("msg", [P, SLOTS, GF])
        r_idx = sb("r_idx", [P, 1], I32)
        r_row = sb("r_row", [P, d])
        r_ea = sb("r_ea", [P, d])
        r_eat = sb("r_eat", [d, P])
        r_pre = sb("r_pre", [P, d])
        r_msg = sb("r_msg", [P, d])
        r_key = sb("r_key", [P, 1])
        r_onehot = sb("r_onehot", [P, BANK])
        acc = sb("acc", [d, SWEEPS * BANK])
        nodes = sb("nodes", [P, blocks * d])
        stack = sb("stack", [P, CF])
        hid = sb("hid", [P, SLOTS, CF])
        v = sb("v", [P, CF])
        sq = sb("sq", [P, SLOTS, CF])
        total = sb("total", [P, CHUNK])
        var = sb("var", [P, CHUNK])
        std = sb("std", [P, CHUNK])
        rstd = sb("rstd", [P, CHUNK])
        x1c = sb("x1c", [P, SLOTS, CF])
        x1t = sb("x1t", [P, SLOTS, CF])
        yc = sb("yc", [P, SLOTS, CF])
        var1 = sb("var1", [P, blocks])
        std1 = sb("std1", [P, blocks])
        rstd1 = sb("rstd1", [P, blocks])

        psum = ctx.enter_context(nc.psum_tensor("psum", [P, 8, BANK], F32))

        def bank(k):
            return psum[:, k, :]

        def two_banks(k):
            return psum[:, k:k + 2, :].rearrange("p a b -> p (a b)")

        windows = [bank(0)[0:d, 0:WINDOW], bank(1)[0:d, 0:WINDOW]]
        eat_ps = [bank(2), bank(3)]
        msg_ps = [bank(4), bank(5)]
        r_window_ps = bank(6)[0:d, :]
        r_eat_ps = bank(7)[0:d, 0:P]
        r_pre_ps = bank(7)[:, P:P + d]
        wide_ps = [two_banks(0), two_banks(2)]
        node_ps = [two_banks(4), two_banks(6)]
        base_ps = bank(7)[:, 256:256 + TB]
        row_ps = bank(7)[0:1, 288:288 + n_groups]
        flag_ps = bank(7)[0:1, 256:256 + P]

        src_landed, dst_landed = sem("src_landed"), sem("dst_landed")
        weights_landed, weights_zeroed = sem("weights_landed"), sem("weights_zeroed")
        pads_set = sem("index_pads_set")
        iota_made, ident_zeroed, ident_made = sem("iota_made"), sem("ident_zeroed"), sem("ident_made")
        spread_made, eps_made = sem("spread_made"), sem("one_eps_made")
        src_as_f, dst_as_f = sem("src_as_float"), sem("dst_as_float")
        src_t, src_copied = sem("src_transposed"), sem("src_copied")
        base_summed, base_made = sem("base_summed"), sem("base_made")
        loc_made, loc_t, loc_copied = sem("loc_made"), sem("loc_transposed"), sem("loc_copied")
        rows_summed, base_row_made = sem("base_rows_summed"), sem("base_row_made")
        left_step, flag_t, flag_made = sem("left_step"), sem("flag_transposed"), sem("flag_made")
        x_landed = [sem(f"x_landed{c}") for c in range(chunks)]
        x_t, acc_started, b2_added = sem("x_transposed"), sem("acc_started"), sem("b2_added")

        class Names:
            pass

        def edge_sems(n):
            s = Names()
            s.idx_ready = sems(f"l{n}_idx_ready")
            s.gathered = sems(f"l{n}_gathered")
            s.onehot_ready = sems(f"l{n}_onehot_ready")
            s.windows_done = sems(f"l{n}_windows_done")
            s.acc_added = sem(f"l{n}_acc_added")
            s.r_start = sem(f"l{n}_r_left_transposed")
            s.r_left = sem(f"l{n}_r_left_copied")
            s.r_idx = sem(f"l{n}_r_idx")
            s.r_gathered = sem(f"l{n}_r_gathered")
            s.r_key = sem(f"l{n}_r_key")
            s.r_onehot = sem(f"l{n}_r_onehot")
            s.r_window = sem(f"l{n}_r_window")
            s.r_added = sem(f"l{n}_r_added")
            return s

        L = [edge_sems(0), edge_sems(1)]
        ea_landed, ea_t = sems("ea_landed"), sems("ea_transposed")
        eat_ready, edge_part = sems("eat_ready"), sems("edge_part_summed")
        pre_ready, msg_ready = sems("pre_ready"), sems("msg_ready")
        r_ea_landed, r_ea_t, r_eat_ready = sem("r_ea_landed"), sem("r_ea_transposed"), sem("r_eat_ready")
        r_part, r_pre_ready, r_msg_ready = sem("r_part_summed"), sem("r_pre_ready"), sem("r_msg_ready")

        def node_sems(n):
            s = Names()
            s.stacked = sem(f"n{n}_stacked")
            s.up_done = sem(f"n{n}_up_done")
            s.hid_ready = sem(f"n{n}_hid_ready")
            s.out_done = sem(f"n{n}_out_done")
            s.step = sem(f"n{n}_step")
            return s

        N0, N1 = node_sems(0), node_sems(1)
        STEPS0, STEPS1 = 7, 3
        std_ready, x1_t, x1t_ready = sem("std_ready"), sem("x1_transposed"), sem("x1t_ready")
        x1_kept, acc_set = sem("x1_kept"), sem("acc_set")
        y_summed, y_ready, y_stored = sem("y_summed"), sem("y_ready"), sems("y_stored")
        sq_ready, var_ready, rstd_ready = sem("sq_ready"), sem("var_ready"), sem("rstd_ready")
        out_ready, out_stored = sem("out_ready"), sem("out_stored")
        W_LOADS = 17

        def tile_at(i, h):
            return i * (SLOTS * GROUP) + h * GROUP

        def over_groups(eng, body):
            for h in range(SLOTS):
                body(0, h, True)
            with eng.Fori(1, iters) as i:
                for h in range(SLOTS):
                    body(i, h, False)

        def over_chunks(eng, body):
            body(0, 0)
            body(1, 1)
            with eng.Fori(1, (chunks - 1) // 2) as i:
                body(2 * i, 0)
                body(2 * i + 1, 1)
            body(chunks - 1, 0)

        def reused(c):
            return not (isinstance(c, int) and c < SLOTS)

        def last_chunk(c):
            return isinstance(c, int) and c == chunks - 1

        def alone(eng):
            eng.nop(nofuse=True)

        def if_leftover(eng, wait_on, body):
            eng.wait_ge(flag_made, 1)
            flag = eng.value_load(left_flag[0:1, 0:1], min_val=0, max_val=1)
            with eng.If(flag):
                body()
            with eng.Else():
                eng.nop()

        def over_tiles(eng, body):
            with eng.Fori(0, full_tiles) as t:
                body(t, P)
            body(full_tiles, last_edges)

        block = ctx.enter_context(nc.Block())

        @block.sync
        def _(sp):
            whole = full_tiles // P
            rest = full_tiles - whole * P
            sp.wait_ge(pads_set, 3)
            for raw, ap, s in ((src_raw, src, src_landed), (dst_raw, dst, dst_landed)):
                sp.dma_start(raw[:, 0:whole * P].rearrange("p (k e) -> p k e", e=P),
                             ap[0:whole * P * P].rearrange("(k p e) -> p k e", p=P, e=P)).then_inc(s, 16)
                sp.dma_start(raw[0:rest, whole * P:(whole + 1) * P],
                             ap[whole * P * P:full_tiles * P].rearrange("(p e) -> p e", e=P)).then_inc(s, 16)
                sp.dma_start(raw[rest:rest + 1, whole * P:whole * P + last_edges],
                             ap[full_tiles * P:n_edges].rearrange("(p e) -> p e", p=1)).then_inc(s, 16)
            for c in range(chunks):
                nb = CHUNK - 1 if c == chunks - 1 else CHUNK
                sp.dma_start(nodes[:, c * CF:c * CF + nb * d].rearrange("p (b f) -> p b f", f=d),
                             x[c * CN:c * CN + nb * P, :].rearrange("(b p) f -> p b f", p=P)
                             ).then_inc(x_landed[c], 16)
            sp.dma_start(nodes[0:last_rows, (blocks - 1) * d:], x[n_nodes - last_rows:n_nodes, :]
                         ).then_inc(x_landed[chunks - 1], 16)
            sp.wait_ge(weights_zeroed, 5)
            for diag, w in ((w1_diag, w1), (w2_diag, w2), (wnode_diag, w_msg[0:d, :]),
                            (wedge_diag, w_msg[d:2 * d, :]), (wupd_diag, w_upd)):
                sp.dma_start(diag[0:d, 0:d], w).then_inc(weights_landed, 16)
                sp.dma_start(diag[d:P, d:P], w).then_inc(weights_landed, 16)
            for col, b in ((b1_col, b1), (bupd_col, b_upd)):
                sp.dma_start(col[0:d, :], b.rearrange("(f a) -> f a", a=1)).then_inc(weights_landed, 16)
                sp.dma_start(col[d:P, :], b.rearrange("(f a) -> f a", a=1)).then_inc(weights_landed, 16)
            for many, b in ((b2_rows, b2), (bmsg_rows, b_msg)):
                sp.dma_start(many[:, :], b.rearrange("(a f) -> a f", a=1).to_broadcast([P, d])
                             ).then_inc(weights_landed, 16)
            sp.dma_start(one_eps[:, :], eps.rearrange("(f a) -> f a", a=1).to_broadcast([P, 1])
                         ).then_inc(weights_landed, 16)

            def store_y(c, h):
                sp.wait_ge(y_ready, c + 1)
                sp.dma_start(msg_table[bass.ds(c * CN, CN), :].rearrange("(b p) f -> p b f", p=P),
                             yc[:, h, :].rearrange("p (b f) -> p b f", f=d)).then_inc(y_stored[h], 16)

            over_chunks(sp, store_y)

            def load_ea(i, h, first, n=GROUP):
                if not first:
                    sp.wait_ge(ea_t[h], i)
                sp.dma_start(ea[:, h, 0:n, :],
                             edge_attr[bass.ds(tile_at(i, h) * P, n * P), :].rearrange("(t p) f -> p t f", p=P)
                             ).then_inc(ea_landed[h], 16)

            for h in range(SLOTS):
                load_ea(0, h, True)
            with sp.Fori(1, iters - 1) as i:
                for h in range(SLOTS):
                    load_ea(i, h, False)
            load_ea(iters - 1, 0, False)
            n = full_tiles - tile_at(iters - 1, 1)
            load_ea(iters - 1, 1, False, n)
            sp.dma_start(ea[0:last_edges, 1, n, :], edge_attr[full_tiles * P:n_edges, :]
                         ).then_inc(ea_landed[1], 16)

            def leftover():
                def body(t, n):
                    sp.wait_ge(L[1].r_added, t * SWEEPS + 1)
                    sp.dma_start(r_ea[0:n, :], edge_attr[bass.ds(t * P, n), :]).then_inc(r_ea_landed, 16)
                over_tiles(sp, body)

            if_leftover(sp, None, leftover)

            for c in range(chunks):
                nb = CHUNK - 1 if c == chunks - 1 else CHUNK
                sp.wait_ge(out_ready, c + 1)
                sp.dma_start(out[c * CN:c * CN + nb * P, :].rearrange("(b p) f -> p b f", p=P),
                             nodes[:, c * CF:c * CF + nb * d].rearrange("p (b f) -> p b f", f=d)
                             ).then_inc(out_stored, 16)
            sp.dma_start(out[n_nodes - last_rows:n_nodes, :], nodes[0:last_rows, (blocks - 1) * d:]
                         ).then_inc(out_stored, 16)
            sp.wait_ge(out_stored, 16 * (chunks + 1))

        @block.gpsimd
        def _(pool):
            nc.gpsimd.memset(ident[:, :], 0.0).then_inc(ident_zeroed, 1)
            pool.wait_ge(ident_zeroed, 1)
            nc.gpsimd.affine_select(out=ident[:, :], in_=ident[:, :], compare_op=ALU.not_equal, fill=1.0,
                                    base=0, pattern=[[-1, P]], channel_multiplier=1).then_inc(ident_made, 1)
            nc.gpsimd.iota(iota_i[:, :], pattern=[[1, BANK]], base=0, channel_multiplier=0).then_inc(iota_made, 1)

            def gather_from(table, s, rows_used):
                def body(i, h, first):
                    if not first:
                        pool.wait_ge(rows_used[h], i)
                    pool.wait_ge(s.idx_ready[h], i + 1)
                    alone(pool)
                    for k in range(GROUP):
                        pool.indirect_dma_start(
                            out=rows[:, h, k * d:(k + 1) * d], out_offset=None, in_=table,
                            in_offset=bass.IndirectOffsetOnAxis(ap=idx_ring[:, h, k:k + 1], axis=0),
                        ).then_inc(s.gathered[h], 16)
                return body

            def leftover_from(table, s):
                def body(t, n):
                    pool.wait_ge(s.r_added, t * SWEEPS + 1)
                    nc.gpsimd.tensor_copy(r_idx[:, :], src_idx[:, bass.ds(t, 1)]).then_inc(s.r_idx, 1)
                    pool.wait_ge(s.r_idx, t + 1)
                    alone(pool)
                    pool.indirect_dma_start(
                        out=r_row[:, :], out_offset=None, in_=table,
                        in_offset=bass.IndirectOffsetOnAxis(ap=r_idx[:, 0:1], axis=0)).then_inc(s.r_gathered, 16)
                return lambda: over_tiles(pool, body)

            over_groups(pool, gather_from(x[:, :], L[0], L[0].windows_done))
            if_leftover(pool, L[0], leftover_from(x[:, :], L[0]))

            def keep_x1(c, h):
                pool.wait_ge(N0.step, STEPS0 * c + STEPS0)
                nc.gpsimd.tensor_copy(nodes[:, bass.ds(c * CF, CF)], x1c[:, h, :]).then_inc(x1_kept, 1)

            over_chunks(pool, keep_x1)
            pool.wait_ge(y_stored[0], 16 * 4)
            pool.wait_ge(y_stored[1], 16 * 3)
            over_groups(pool, gather_from(msg_table[:, :], L[1], pre_ready))
            if_leftover(pool, L[1], leftover_from(msg_table[:, :], L[1]))

        @block.scalar
        def _(act):
            def copy_src(q):
                nb = min(4, TB - 4 * q)
                act.wait_ge(src_t, q + 1)
                nc.scalar.copy(src_idx[:, 4 * q * P:(4 * q + nb) * P], bank(q)[:, 0:nb * P]).then_inc(src_copied, 1)

            def copy_idx(s, i, h, first):
                if not first:
                    act.wait_ge(s.gathered[h], 16 * GROUP * i)
                nc.scalar.copy(idx_ring[:, h, :], src_idx[:, bass.ds(tile_at(i, h), GROUP)]
                               ).then_inc(s.idx_ready[h], 1)

            copy_src(0)
            act.wait_ge(src_copied, 1)
            for h in range(SLOTS):
                copy_idx(L[0], 0, h, True)
            for q in range(1, 4):
                copy_src(q)

            def blocks_of(c, parity):
                return acc[:, bass.ds(c * CN, CN)].rearrange("p (j q n) -> p j q n", q=2, n=P)[:, :, parity, :]

            def pair_half(t, parity):
                return t[parity * d:(parity + 1) * d, 0:CF].rearrange("p (j n) -> p j n", n=P)

            for c in range(chunks):
                act.wait_ge(x_t, c + 1)
                for parity in range(2):
                    last = nc.scalar.copy(blocks_of(c, parity), pair_half(node_ps[c % 2], parity))
                last.then_inc(acc_started, 1)

            act.wait_ge(src_copied, 4)
            with act.Fori(1, iters) as i:
                for h in range(SLOTS):
                    copy_idx(L[0], i, h, False)

            act.wait_ge(eps_made, 1)
            act.wait_ge(L[0].acc_added, n_groups)
            if_leftover(act, L[0], lambda: act.wait_ge(L[0].r_added, tiles * SWEEPS + 1))

            def stack_pairs(s, c):
                if not (isinstance(c, int) and c == 0):
                    act.wait_ge(s.up_done, c)
                for parity in range(2):
                    last = nc.scalar.copy(pair_half(stack, parity), blocks_of(c, parity))
                last.then_inc(s.stacked, 1)

            def hidden(s, func, bias, c, h):
                act.wait_ge(s.up_done, c + 1)
                if reused(c):
                    act.wait_ge(s.out_done, c - 1)
                nc.scalar.activation(hid[:, h, :].rearrange("p (a b) -> p a b", a=2),
                                     wide_ps[h].rearrange("p (a b) -> p a b", a=2)[:, :, 0:HALF], func, bias=bias
                                     ).then_inc(s.hid_ready, 1)

            def root0(c):
                act.wait_ge(N0.step, STEPS0 * c + 5)
                nc.scalar.activation(std[:, :], var[:, :], ACT.Sqrt, bias=ln_eps[:, 0:1], scale=1.0 / d
                                     ).then_inc(std_ready, 1)

            def layer0(c, h):
                if not last_chunk(c):
                    stack_pairs(N0, c + 1)
                root0(c)
                if not last_chunk(c):
                    hidden(N0, ACT.Relu, b1_col[:, 0:1], c + 1, 1 - h)
                act.wait_ge(x1_t, c + 1)
                if reused(c):
                    act.wait_ge(y_summed, c - 1)
                nc.scalar.copy(x1t[:, h, :], wide_ps[h][:, 0:CF]).then_inc(x1t_ready, 1)
                for parity in range(2):
                    last = nc.scalar.activation(blocks_of(c, parity), pair_half(wide_ps[h], parity), ACT.Copy,
                                                scale=one_eps[parity * d:(parity + 1) * d, 0:1])
                last.then_inc(acc_set, 1)

            stack_pairs(N0, 0)
            hidden(N0, ACT.Relu, b1_col[:, 0:1], 0, 0)
            over_chunks(act, layer0)

            def edge(i, h, first, last=False):
                if h == 0:
                    copy_idx(L[1], i, 1, first)
                elif not last:
                    copy_idx(L[1], i + 1, 0, False)
                act.wait_ge(ea_t[h], i + 1)
                if not first:
                    act.wait_ge(edge_part[h], i)
                nc.scalar.copy(eat[:, h, :], eat_ps[h]).then_inc(eat_ready[h], 1)
                act.wait_ge(pre_ready[h], i + 1)
                if not first:
                    act.wait_ge(L[1].windows_done[h], i)
                nc.scalar.activation(msg[:, h, :], pre[:, h, :], ACT.Gelu_apprx_tanh).then_inc(msg_ready[h], 1)

            copy_idx(L[1], 0, 0, True)
            for h in range(SLOTS):
                edge(0, h, True)
            with act.Fori(1, iters - 1) as i:
                for h in range(SLOTS):
                    edge(i, h, False)
            for h in range(SLOTS):
                edge(iters - 1, h, False, last=True)

            def leftover1():
                def body(t, n):
                    act.wait_ge(r_ea_t, t + 1)
                    nc.scalar.copy(r_eat[:, :], r_eat_ps).then_inc(r_eat_ready, 1)
                    act.wait_ge(r_pre_ready, t + 1)
                    nc.scalar.activation(r_msg[:, :], r_pre[:, :], ACT.Gelu_apprx_tanh).then_inc(r_msg_ready, 1)
                over_tiles(act, body)
                act.wait_ge(L[1].r_added, tiles * SWEEPS + 1)

            act.wait_ge(L[1].acc_added, n_groups)
            if_leftover(act, L[1], leftover1)

            def square(c, h):
                act.wait_ge(N1.step, STEPS1 * c + STEPS1)
                if reused(c):
                    act.wait_ge(var_ready, c - 1)
                nc.scalar.square(sq[:, h, :], nodes[:, bass.ds(c * CF, CF)]).then_inc(sq_ready, 1)

            def layer1(c, h):
                if not last_chunk(c):
                    stack_pairs(N1, c + 1)
                    hidden(N1, ACT.Gelu_apprx_tanh, bupd_col[:, 0:1], c + 1, 1 - h)
                square(c, h)

            stack_pairs(N1, 0)
            hidden(N1, ACT.Gelu_apprx_tanh, bupd_col[:, 0:1], 0, 0)
            over_chunks(act, layer1)
            act.wait_ge(var_ready, chunks)
            nc.scalar.activation(std1[:, :], var1[:, :], ACT.Sqrt, bias=ln_eps[:, 0:1], scale=1.0 / d
                                 ).then_inc(std_ready, 1)

        @block.vector
        def _(dve):
            short = (TB - 1) * P
            nc.vector.memset(src_raw[:, short:], 0).then_inc(pads_set, 1)
            nc.vector.memset(dst_raw[:, short:], -1).then_inc(pads_set, 1)
            nc.vector.memset(nodes[:, (blocks - 1) * d:], 0.0).then_inc(pads_set, 1)
            for w in (w1_diag, w2_diag, wnode_diag, wedge_diag, wupd_diag):
                nc.vector.memset(w[:, :], 0.0).then_inc(weights_zeroed, 1)
            nc.vector.memset(ln_eps[:, :], LN_EPS)
            nc.vector.memset(acc[:, blocks * P:], 0.0)
            dve.wait_ge(src_landed, 48)
            nc.vector.tensor_copy(src_f[:, :], src_raw[:, :]).then_inc(src_as_f, 1)
            dve.wait_ge(dst_landed, 48)
            nc.vector.tensor_copy(dst_f[:, :], dst_raw[:, :]).then_inc(dst_as_f, 1)
            dve.wait_ge(ident_made, 1)
            nc.vector.tensor_copy(spread[:, :].rearrange("p (g k) -> p g k", k=GROUP),
                                  ident[:, ::GROUP].rearrange("p (g a) -> p g a", a=1)
                                  .to_broadcast([P, P // GROUP, GROUP])).then_inc(spread_made, 1)

            def by_block(t):
                return t.rearrange("p (k e) -> p k e", e=P)

            dve.wait_ge(base_summed, 1)
            nc.vector.tensor_scalar(base_col[:, :], base_ps, 0.0, None, ALU.max).then_inc(base_made, 1)
            dve.wait_ge(base_made, 1)
            dve.wait_ge(src_t, 1)
            dve.wait_ge(dst_as_f, 1)
            dve.wait_ge(src_as_f, 1)
            nc.vector.tensor_tensor(by_block(loc_f), by_block(dst_f[:, :]),
                                    base_col[:, :].rearrange("p (k a) -> p k a", a=1).to_broadcast([P, TB, P]),
                                    ALU.subtract).then_inc(loc_made, 1)
            dve.wait_ge(iota_made, 1)
            nc.vector.tensor_copy(iota_f[:, :], iota_i[:, :])
            dve.wait_ge(rows_summed, 1)
            nc.vector.tensor_copy(base_row[:, :], row_ps).then_inc(base_row_made, 1)
            for q in range(4):
                nb = min(4, TB - 4 * q)
                dve.wait_ge(loc_t, q + 1)
                nc.vector.tensor_copy(dst_loc[:, 4 * q * P:(4 * q + nb) * P], bank(4 + q)[:, 0:nb * P]
                                      ).then_inc(loc_copied, 1)
            nc.vector.tensor_scalar(left_f, loc_f, float(WINDOW), None, ALU.is_ge).then_inc(left_step, 1)
            dve.wait_ge(left_step, 1)
            nc.vector.scalar_tensor_tensor(out=left_f, in0=loc_f, scalar=0.0, in1=left_f,
                                           op0=ALU.is_lt, op1=ALU.add).then_inc(left_step, 1)
            dve.wait_ge(left_step, 2)
            nc.vector.scalar_tensor_tensor(out=left_f, in0=dst_f[:, :], scalar=0.0, in1=left_f,
                                           op0=ALU.is_ge, op1=ALU.mult).then_inc(left_step, 1)
            dve.wait_ge(left_step, 3)
            nc.vector.tensor_reduce(left_max[:, :], left_f, AX.X, ALU.max).then_inc(left_step, 1)
            nc.vector.scalar_tensor_tensor(out=dst_f[:, :], in0=dst_f[:, :], scalar=1.0, in1=left_f,
                                           op0=ALU.add, op1=ALU.mult).then_inc(left_step, 1)
            dve.wait_ge(flag_t, 1)
            nc.vector.tensor_reduce(left_flag[:, :], flag_ps, AX.X, ALU.max).then_inc(flag_made, 1)
            for s in L:
                dve.nop().then_inc(s.r_added, 1)

            dve.wait_ge(weights_landed, 16 * W_LOADS)
            nc.vector.tensor_scalar(one_eps[:, :], one_eps[:, :], 1.0, None, ALU.add).then_inc(eps_made, 1)
            dve.wait_ge(x_t, chunks)
            for c in range(chunks):
                part = nodes[:, c * CF:(c + 1) * CF].rearrange("p (b f) -> p b f", f=d)
                nc.vector.tensor_tensor(part, part, b2_rows[:, :].rearrange("p (a f) -> p a f", a=1)
                                        .to_broadcast([P, CHUNK, d]), ALU.add).then_inc(b2_added, 1)

            dve.wait_ge(base_row_made, 1)
            dve.wait_ge(loc_copied, 4)

            def make_onehot(s, i, h, first):
                if not first:
                    dve.wait_ge(s.windows_done[h], i)
                nc.vector.tensor_tensor(
                    onehot[:, h, :, :],
                    iota_f[:, 0:WINDOW].rearrange("p (a n) -> p a n", a=1).to_broadcast([P, GROUP, WINDOW]),
                    dst_loc[:, bass.ds(tile_at(i, h), GROUP)].rearrange("p (g a) -> p g a", a=1)
                    .to_broadcast([P, GROUP, WINDOW]), ALU.is_equal).then_inc(s.onehot_ready[h], 1)

            def add_window(s, i, h, first):
                g = i * SLOTS + h
                base = dve.value_load(base_row[0:1, bass.ds(g, 1)], min_val=0, max_val=n_nodes - 1)
                dve.wait_ge(s.windows_done[h], i + 1)
                if not (first and h == 0):
                    dve.wait_ge(s.acc_added, g)
                at = acc[:, bass.ds(base, WINDOW)]
                nc.vector.tensor_tensor(at, at, windows[h], ALU.add).then_inc(s.acc_added, 1)

            def edge0(i, h, first):
                make_onehot(L[0], i, h, first)
                if first and h == 0:
                    dve.wait_ge(acc_started, chunks)
                add_window(L[0], i, h, first)

            over_groups(dve, edge0)

            def leftover(s, before):
                def body(t, n):
                    dve.wait_ge(s.r_added, t * SWEEPS + 1)
                    before(t)
                    nc.vector.tensor_scalar(r_key[:, :], dst_left[:, bass.ds(t, 1)], 1.0, None, ALU.subtract
                                            ).then_inc(s.r_key, 1)
                    with dve.Fori(0, SWEEPS) as w:
                        n_done = t * SWEEPS + w
                        dve.wait_ge(s.r_added, n_done + 1)
                        dve.wait_ge(s.r_key, t * (SWEEPS + 1) + w + 1)
                        nc.vector.tensor_scalar(r_onehot[:, :], iota_f[:, :], r_key[:, 0:1], None, ALU.is_equal
                                                ).then_inc(s.r_onehot, 1)
                        dve.wait_ge(s.r_onehot, n_done + 1)
                        nc.vector.tensor_scalar(r_key[:, :], r_key[:, :], float(BANK), None, ALU.subtract
                                                ).then_inc(s.r_key, 1)
                        dve.wait_ge(s.r_window, n_done + 1)
                        at = acc[:, bass.ds(w * BANK, BANK)]
                        nc.vector.tensor_tensor(at, at, r_window_ps, ALU.add).then_inc(s.r_added, 1)
                over_tiles(dve, body)

            def leftover0():
                for q in range(4):
                    nb = min(4, TB - 4 * q)
                    dve.wait_ge(L[0].r_start, q + 1)
                    nc.vector.tensor_copy(dst_left[:, 4 * q * P:(4 * q + nb) * P], bank(6 + q % 2)[:, 0:nb * P]
                                          ).then_inc(L[0].r_left, 1)
                dve.wait_ge(L[0].r_left, 4)
                dve.wait_ge(L[0].acc_added, n_groups)
                leftover(L[0], lambda t: None)

            if_leftover(dve, L[0], leftover0)

            def three(t):
                return t.rearrange("p (b f) -> p b f", f=d)

            def over_f(t):
                return t.rearrange("p (b a) -> p b a", a=1).to_broadcast([P, CHUNK, d])

            def center(s, steps, c, h, vc, resid):
                dve.wait_ge(s.out_done, c + 1)
                if not (isinstance(c, int) and c == 0):
                    dve.wait_ge(s.step, steps * c)
                nc.vector.tensor_tensor(vc, node_ps[h][:, 0:CF], resid, ALU.add).then_inc(s.step, 1)
                dve.wait_ge(s.step, steps * c + 1)
                alone(dve)
                nc.vector.tensor_reduce(total[:, :], three(vc), AX.X, ALU.add).then_inc(s.step, 1)
                dve.wait_ge(s.step, steps * c + 2)
                nc.vector.scalar_tensor_tensor(out=three(vc), in0=over_f(total[:, :]), scalar=-1.0 / d,
                                               in1=three(vc), op0=ALU.mult, op1=ALU.add).then_inc(s.step, 1)

            def norm0(c, h):
                center(N0, STEPS0, c, h, v[:, :], nodes[:, bass.ds(c * CF, CF)])
                dve.wait_ge(N0.step, STEPS0 * c + 3)
                nc.vector.tensor_tensor(sq[:, 0, :], v[:, :], v[:, :], ALU.mult).then_inc(N0.step, 1)
                dve.wait_ge(N0.step, STEPS0 * c + 4)
                nc.vector.tensor_reduce(var[:, :], three(sq[:, 0, :]), AX.X, ALU.add).then_inc(N0.step, 1)
                dve.wait_ge(std_ready, c + 1)
                nc.vector.reciprocal(rstd[:, :], std[:, :]).then_inc(N0.step, 1)
                dve.wait_ge(N0.step, STEPS0 * c + 6)
                if reused(c):
                    dve.wait_ge(x1_t, c - 1)
                    dve.wait_ge(x1_kept, c - 1)
                nc.vector.tensor_tensor(three(x1c[:, h, :]), three(v[:, :]), over_f(rstd[:, :]), ALU.mult
                                        ).then_inc(N0.step, 1)

            def add_bmsg(c, h, use):
                dve.wait_ge(y_summed, c + 1)
                if reused(c):
                    dve.wait_ge(y_stored[h], 16 * use)
                nc.vector.tensor_tensor(three(yc[:, h, :]), three(node_ps[h][:, 0:CF]),
                                        bmsg_rows[:, :].rearrange("p (a f) -> p a f", a=1)
                                        .to_broadcast([P, CHUNK, d]), ALU.add).then_inc(y_ready, 1)

            def layer0(c, h, use):
                if not last_chunk(c):
                    norm0(c + 1, 1 - h)
                add_bmsg(c, h, use)

            dve.wait_ge(b2_added, chunks)
            norm0(0, 0)
            layer0(0, 0, 0)
            layer0(1, 1, 0)
            with dve.Fori(1, (chunks - 1) // 2) as i:
                layer0(2 * i, 0, i)
                layer0(2 * i + 1, 1, i)
            layer0(chunks - 1, 0, (chunks - 1) // 2)

            def edge1(i, h, first):
                make_onehot(L[1], i, h, first)
                dve.wait_ge(edge_part[h], i + 1)
                dve.wait_ge(L[1].gathered[h], 16 * GROUP * (i + 1))
                if not first:
                    dve.wait_ge(msg_ready[h], i)
                nc.vector.tensor_tensor(pre[:, h, :], msg_ps[h], rows[:, h, :], ALU.add).then_inc(pre_ready[h], 1)
                add_window(L[1], i, h, first)

            dve.wait_ge(acc_set, chunks)
            over_groups(dve, edge1)

            def before1(t):
                dve.wait_ge(r_part, t + 1)
                dve.wait_ge(L[1].r_gathered, 16 * (t + 1))
                nc.vector.tensor_tensor(r_pre[:, :], r_pre_ps, r_row[:, :], ALU.add).then_inc(r_pre_ready, 1)

            def leftover1():
                dve.wait_ge(L[1].acc_added, n_groups)
                leftover(L[1], before1)

            if_leftover(dve, L[1], leftover1)

            dve.wait_ge(x1_kept, chunks)

            def center1(c, h):
                part = nodes[:, bass.ds(c * CF, CF)]
                center(N1, STEPS1, c, h, part, part)

            def sum_squares(c, h):
                dve.wait_ge(sq_ready, c + 1)
                alone(dve)
                nc.vector.tensor_reduce(var1[:, bass.ds(c * CHUNK, CHUNK)], three(sq[:, h, :]), AX.X, ALU.add
                                        ).then_inc(var_ready, 1)

            def layer1(c, h):
                if not last_chunk(c):
                    center1(c + 1, 1 - h)
                sum_squares(c, h)

            center1(0, 0)
            over_chunks(dve, layer1)
            dve.wait_ge(std_ready, chunks + 1)
            nc.vector.reciprocal(rstd1[:, :], std1[:, :]).then_inc(rstd_ready, 1)
            dve.wait_ge(rstd_ready, 1)
            for c in range(chunks):
                part = three(nodes[:, c * CF:(c + 1) * CF])
                nc.vector.tensor_tensor(part, part, over_f(rstd1[:, c * CHUNK:(c + 1) * CHUNK]), ALU.mult
                                        ).then_inc(out_ready, 1)

        @block.tensor
        def _(pe):
            def block_t(out_bank, q, source, signal):
                nb = min(4, TB - 4 * q)
                for k in range(nb):
                    last = nc.tensor.transpose(out_bank[:, k * P:(k + 1) * P],
                                               source[:, (4 * q + k) * P:(4 * q + k + 1) * P], ident[:, :])
                last.then_inc(signal, 1)

            pe.wait_ge(ident_made, 1)
            pe.wait_ge(src_as_f, 1)
            for q in range(4):
                block_t(bank(q), q, src_f, src_t)
            pe.wait_ge(dst_as_f, 1)
            pe.wait_ge(spread_made, 1)
            nc.tensor.matmul(base_ps, spread[:, :], dst_f[:, ::P], start=True, stop=True).then_inc(base_summed, 1)
            pe.wait_ge(base_made, 1)
            for k in range(TB):
                last = nc.tensor.matmul(row_ps[:, k * P // GROUP:(k + 1) * P // GROUP], base_col[:, k:k + 1],
                                        ident[:, ::GROUP], start=True, stop=True)
            last.then_inc(rows_summed, 1)
            pe.wait_ge(loc_made, 1)
            for q in range(4):
                if q == 3:
                    pe.wait_ge(base_row_made, 1)
                block_t(bank(4 + q), q, loc_f, loc_t)

            pe.wait_ge(loc_copied, 4)
            for c in range(chunks):
                pe.wait_ge(x_landed[c], 32 if c == chunks - 1 else 16)
                if c >= 2:
                    pe.wait_ge(acc_started, c - 1)
                for j in range(pairs):
                    last = nc.tensor.transpose(node_ps[c % 2][:, j * P:(j + 1) * P],
                                               nodes[:, c * CF + j * P:c * CF + (j + 1) * P], ident[:, :])
                last.then_inc(x_t, 1)
            pe.wait_ge(acc_started, chunks)
            pe.wait_ge(left_step, 4)
            nc.tensor.transpose(flag_ps, left_max[:, 0:1], ident[:, :]).then_inc(flag_t, 1)

            def sum_group(s, rhs, i, h, first):
                pe.wait_ge(s.onehot_ready[h], i + 1)
                if not first:
                    pe.wait_ge(s.acc_added, (i - 1) * SLOTS + h + 1)
                for k in range(GROUP):
                    last = nc.tensor.matmul(windows[h], rhs[:, h, k * d:(k + 1) * d], onehot[:, h, k, :],
                                            start=k == 0, stop=k == GROUP - 1)
                last.then_inc(s.windows_done[h], 1)

            pe.wait_ge(src_copied, 4)

            def edge0(i, h, first):
                pe.wait_ge(L[0].gathered[h], 16 * GROUP * (i + 1))
                sum_group(L[0], rows, i, h, first)

            over_groups(pe, edge0)

            def sweeps(s, t, rhs):
                alone(pe)
                with pe.Fori(0, SWEEPS) as w:
                    pe.wait_ge(s.r_onehot, t * SWEEPS + w + 1)
                    nc.tensor.matmul(r_window_ps, rhs[:, :], r_onehot[:, :], start=True, stop=True
                                     ).then_inc(s.r_window, 1)

            def leftover0():
                pe.wait_ge(flag_made, 1)
                pe.wait_ge(left_step, 5)
                for q in range(4):
                    if q >= 2:
                        pe.wait_ge(L[0].r_left, q - 1)
                    block_t(bank(6 + q % 2), q, dst_f, L[0].r_start)
                pe.wait_ge(L[0].r_left, 4)

                def body(t, n):
                    pe.wait_ge(L[0].r_gathered, 16 * (t + 1))
                    sweeps(L[0], t, r_row)
                over_tiles(pe, body)

            if_leftover(pe, L[0], leftover0)

            def up(s, w, c, h, free):
                pe.wait_ge(s.stacked, c + 1)
                if reused(c):
                    free(c)
                for a in range(2):
                    last = nc.tensor.matmul(wide_ps[h][:, a * BANK:a * BANK + HALF], w[:, :],
                                            stack[:, a * HALF:(a + 1) * HALF], start=True, stop=True)
                last.then_inc(s.up_done, 1)

            def over_pairs(out_ps, lhsT, w, signal):
                for j in range(pairs):
                    last = nc.tensor.matmul(out_ps[:, j * P:(j + 1) * P], lhsT[:, j * P:(j + 1) * P], w[:, :],
                                            start=True, stop=True)
                last.then_inc(signal, 1)

            def pairs_t(out_ps, source, signal):
                alone(pe)
                for j in range(pairs):
                    last = nc.tensor.transpose(out_ps[:, j * P:(j + 1) * P], source[:, j * P:(j + 1) * P],
                                               ident[:, :])
                last.then_inc(signal, 1)

            def up0(c, h):
                up(N0, w1_diag, c, h, lambda c: pe.wait_ge(acc_set, c - 1))

            def out0(c, h):
                pe.wait_ge(N0.hid_ready, c + 1)
                if reused(c):
                    pe.wait_ge(y_ready, c - 1)
                over_pairs(node_ps[h], hid[:, h, :], w2_diag, N0.out_done)

            def layer0(c, h):
                if not last_chunk(c):
                    up0(c + 1, 1 - h)
                pe.wait_ge(N0.step, STEPS0 * c + STEPS0)
                pairs_t(wide_ps[h], x1c[:, h, :], x1_t)
                if not last_chunk(c):
                    out0(c + 1, 1 - h)
                pe.wait_ge(x1t_ready, c + 1)
                over_pairs(node_ps[h], x1t[:, h, :], wnode_diag, y_summed)

            pe.wait_ge(weights_landed, 16 * W_LOADS)
            up0(0, 0)
            out0(0, 0)
            over_chunks(pe, layer0)
            pe.wait_ge(acc_set, chunks)
            pe.wait_ge(y_ready, chunks)

            def edge1(i, h, first):
                pe.wait_ge(ea_landed[h], 16 * (i + 1) + (16 if isinstance(i, int) and i == iters - 1 and h == 1 else 0))
                if not first:
                    pe.wait_ge(eat_ready[h], i)
                alone(pe)
                for k in range(GROUP // 2):
                    last = nc.tensor.transpose(eat_ps[h][:, k * P:(k + 1) * P],
                                               ea[:, h, 2 * k:2 * k + 2, :].rearrange("p a f -> p (a f)"), ident[:, :])
                last.then_inc(ea_t[h], 1)
                pe.wait_ge(eat_ready[h], i + 1)
                if not first:
                    pe.wait_ge(pre_ready[h], i)
                for k in range(GROUP // 2):
                    last = nc.tensor.matmul(msg_ps[h][:, k * P:(k + 1) * P], eat[:, h, k * P:(k + 1) * P],
                                            wedge_diag[:, :], start=True, stop=True)
                last.then_inc(edge_part[h], 1)
                pe.wait_ge(msg_ready[h], i + 1)
                sum_group(L[1], msg, i, h, first)

            for h in range(SLOTS):
                edge1(0, h, True)
            with pe.Fori(1, iters - 1) as i:
                for h in range(SLOTS):
                    edge1(i, h, False)
            for h in range(SLOTS):
                edge1(iters - 1, h, False)

            def leftover1():
                def body(t, n):
                    pe.wait_ge(r_ea_landed, 16 * (t + 1))
                    alone(pe)
                    nc.tensor.transpose(r_eat_ps, r_ea[:, :], ident[:, :]).then_inc(r_ea_t, 1)
                    pe.wait_ge(r_eat_ready, t + 1)
                    nc.tensor.matmul(r_pre_ps, r_eat[:, :], wedge_diag[0:d, 0:d], start=True, stop=True
                                     ).then_inc(r_part, 1)
                    pe.wait_ge(r_msg_ready, t + 1)
                    sweeps(L[1], t, r_msg)
                over_tiles(pe, body)

            if_leftover(pe, L[1], leftover1)

            def up1(c, h):
                up(N1, wupd_diag, c, h, lambda c: pe.wait_ge(N1.hid_ready, c - 1))

            def out1(c, h):
                pe.wait_ge(N1.hid_ready, c + 1)
                if reused(c):
                    pe.wait_ge(N1.step, STEPS1 * (c - 2) + 1)
                pairs_t(node_ps[h], hid[:, h, :], N1.out_done)

            def layer1(c, h):
                if not last_chunk(c):
                    up1(c + 1, 1 - h)
                out1(c, h)

            pe.wait_ge(L[1].acc_added, n_groups)
            up1(0, 0)
            over_chunks(pe, layer1)


_INS = ["x", "src", "dst", "edge_attr_64", "L0_gnn_W1", "L0_gnn_b1", "L0_gnn_W2", "L0_gnn_b2",
        "L1_gnn_W_msg", "L1_gnn_b_msg", "L1_gnn_W_upd", "L1_gnn_b_upd", "L1_gnn_eps"]


def kernel(**inputs):
    import numpy as _np
    import concourse.bacc as _bacc
    from concourse import mybir as _mybir
    from concourse.bass_utils import run_bass_kernel_spmd as _run

    nc = _bacc.Bacc("TRN2", target_bir_lowering=False, num_devices=1)
    arrays, args = {}, []
    for name in _INS:
        a = _np.ascontiguousarray(inputs[name])
        arrays[f"in_{name}"] = a
        args.append(nc.dram_tensor(f"in_{name}", a.shape, _mybir.dt.from_np(a.dtype), kind="ExternalInput").ap())
    shape = inputs["x"].shape
    args.append(nc.dram_tensor("out_0", shape, F32, kind="ExternalOutput").ap())
    gnn_kernel(nc, *args)
    r = _run(nc, [arrays], core_ids=[0])
    return r.results[0]["out_0"]
```

```python
from contextlib import ExitStack

import concourse.bass as bass
from concourse import mybir

ALU = mybir.AluOpType
ACT = mybir.ActivationFunctionType
AX = mybir.AxisListType
F32 = mybir.dt.float32
I32 = mybir.dt.int32

P = 128
BANK = 512
SLOTS = 2
GROUP = 8
WINDOW = 96
CHUNK = 14
STEP = 4
LAG = 5
LN_EPS = 1e-5


def gnn_kernel(nc, x, src, dst, edge_attr, w1, b1, w2, b2, w_msg, b_msg, w_upd, b_upd, eps, out):
    n_nodes, d = x.shape
    n_edges = src.shape[0]
    tiles = -(-n_edges // P)
    iters = -(-tiles // (SLOTS * GROUP))
    tiles_pad = iters * SLOTS * GROUP
    n_groups = iters * SLOTS
    last_tiles = tiles - (n_groups - 1) * GROUP
    full_tiles = n_edges // P
    last_edges = n_edges - full_tiles * P
    TB = -(-tiles_pad // P)
    blocks = n_nodes // P + 1
    chunks = blocks // CHUNK
    pairs = CHUNK // 2
    all_pairs = blocks // 2
    STEPS = n_groups // STEP
    in_loop = STEPS - LAG
    REST = all_pairs - in_loop
    turns = in_loop + 1
    last_rows = (n_nodes - (blocks - 2) * P) // 2
    CN = CHUNK * P
    CF = CHUNK * d
    GF = GROUP * d
    SWEEPS = -(-n_nodes // BANK)
    assert blocks == chunks * CHUNK and STEPS * STEP == n_groups and REST * P <= BANK // 2 and n_nodes % 2 == 0 and chunks == 7 and 2 * d == P and TB * P == tiles_pad and TB == 13

    msg_table = nc.dram_tensor("msg_table", [blocks * P, d], F32, kind="Internal").ap()

    with ExitStack() as ctx:
        def sb(name, shape, dt=F32):
            return ctx.enter_context(nc.sbuf_tensor(name, shape, dt))

        def sem(name):
            return ctx.enter_context(nc.semaphore(name))

        def sems(name):
            return [sem(f"{name}{h}") for h in range(SLOTS)]

        iota_i = sb("iota_i", [P, BANK], I32)
        iota_f = sb("iota_f", [P, BANK])
        ident = sb("ident", [P, P])
        spread = sb("spread", [P, P])
        w1_diag = sb("w1_diag", [P, P])
        w2_diag = sb("w2_diag", [P, P])
        wnode_diag = sb("wnode_diag", [P, P])
        wedge_diag = sb("wedge_diag", [P, P])
        wupd_diag = sb("wupd_diag", [P, P])
        b1_col = sb("b1_col", [P, 1])
        bupd_col = sb("bupd_col", [P, 1])
        b2_rows = sb("b2_rows", [P, d])
        bmsg_rows = sb("bmsg_rows", [P, d])
        one_eps = sb("one_eps", [P, 1])
        ln_eps = sb("ln_eps", [P, 1])
        src_raw = sb("src_raw", [P, TB * P], I32)
        dst_raw = sb("dst_raw", [P, TB * P], I32)
        src_f = sb("src_f", [P, TB * P])
        dst_f = sb("dst_f", [P, TB * P])
        loc_f = src_raw[:, :].bitcast(F32)
        left_f = dst_raw[:, :].bitcast(F32)
        left_max = sb("left_max", [P, 1])
        base_col = sb("base_col", [P, TB])
        src_idx = sb("src_idx", [P, TB * P], I32)
        dst_loc = sb("dst_loc", [P, TB * P])
        dst_left = sb("dst_left", [P, TB * P])
        base_row = sb("base_row", [1, n_groups], I32)
        taken_i = sb("taken_i", [1, STEPS + 1, STEP], I32)
        taken = sb("taken", [1, n_groups])
        late = sb("late", [1, 1])
        left_one = sb("left_one", [1, 1])
        irregular = sb("irregular", [1, 1], I32)
        has_leftover = sb("has_leftover", [1, 1], I32)
        idx_ring = sb("idx_ring", [P, SLOTS, GROUP], I32)
        rows = sb("rows", [P, SLOTS, GF])
        onehot = sb("onehot", [P, SLOTS, GROUP, WINDOW])
        ea = sb("ea", [P, SLOTS, GROUP, d])
        eat = sb("eat", [P, SLOTS, GROUP // 2 * P])
        pre = sb("pre", [P, SLOTS, GF])
        msg = sb("msg", [P, SLOTS, GF])
        r_idx = sb("r_idx", [P, 1], I32)
        r_row = sb("r_row", [P, d])
        r_ea = sb("r_ea", [P, d])
        r_eat = sb("r_eat", [d, P])
        r_pre = sb("r_pre", [P, d])
        r_msg = sb("r_msg", [P, d])
        r_key = sb("r_key", [P, 1])
        r_onehot = sb("r_onehot", [P, BANK])
        acc = sb("acc", [d, SWEEPS * BANK])
        nodes = sb("nodes", [P, blocks * d])
        stack = sb("stack", [P, REST * P])
        hid = sb("hid", [P, REST * P])
        v = sb("v", [P, REST * P])
        sq = sb("sq", [P, REST * P])
        total = sb("total", [P, REST * 2])
        var = sb("var", [P, REST * 2])
        std = sb("std", [P, REST * 2])
        rstd = sb("rstd", [P, REST * 2])
        x1 = sb("x1", [P, REST * P])
        x1t = sb("x1t", [P, REST * P])
        y = sb("y", [P, REST * P])
        result = sb("result", [P, REST * P])

        psum = ctx.enter_context(nc.psum_tensor("psum", [P, 8, BANK], F32))

        def bank(k):
            return psum[:, k, :]

        def two_banks(k):
            return psum[:, k:k + 2, :].rearrange("p a b -> p (a b)")

        windows = [bank(0)[0:d, 0:WINDOW], bank(1)[0:d, 0:WINDOW]]
        eat_ps = [bank(2), bank(3)]
        msg_ps = [bank(4), bank(5)]
        r_window_ps = bank(6)[0:d, :]
        r_eat_ps = bank(7)[0:d, 0:P]
        r_pre_ps = bank(7)[:, P:P + d]
        wide_ps = bank(6)
        node_ps = bank(7)
        x_ps = [two_banks(4), two_banks(6)]
        base_ps = bank(7)[:, 256:256 + TB]
        row_ps = bank(7)[0:1, 288:288 + n_groups]
        flag_ps = bank(7)[0:1, 256:256 + P]

        src_landed, dst_landed = sem("src_landed"), sem("dst_landed")
        weights_landed, weights_zeroed = sem("weights_landed"), sem("weights_zeroed")
        pads_set = sem("index_pads_set")
        iota_made, ident_zeroed, ident_made = sem("iota_made"), sem("ident_zeroed"), sem("ident_made")
        spread_made, eps_made = sem("spread_made"), sem("one_eps_made")
        src_as_f, dst_as_f = sem("src_as_float"), sem("dst_as_float")
        src_t, src_copied = sem("src_transposed"), sem("src_copied")
        base_summed, base_made = sem("base_summed"), sem("base_made")
        loc_made, loc_t, loc_copied = sem("loc_made"), sem("loc_transposed"), sem("loc_copied")
        rows_summed, base_row_made = sem("base_rows_summed"), sem("base_row_made")
        left_step, flag_t, flag_made = sem("left_step"), sem("flag_transposed"), sem("flag_made")
        taken_iota, taken_step = sem("taken_iota"), sem("taken_step")
        x_landed = [sem(f"x_landed{c}") for c in range(chunks)]
        x_t, acc_started, b2_added = sem("x_transposed"), sem("acc_started"), sem("b2_added")

        class Names:
            pass

        def edge_sems(n):
            s = Names()
            s.idx_ready = sems(f"l{n}_idx_ready")
            s.gathered = sems(f"l{n}_gathered")
            s.onehot_ready = sems(f"l{n}_onehot_ready")
            s.windows_done = sems(f"l{n}_windows_done")
            s.acc_added = sem(f"l{n}_acc_added")
            s.r_start = sem(f"l{n}_r_left_transposed")
            s.r_left = sem(f"l{n}_r_left_copied")
            s.r_idx = sem(f"l{n}_r_idx")
            s.r_gathered = sem(f"l{n}_r_gathered")
            s.r_key = sem(f"l{n}_r_key")
            s.r_onehot = sem(f"l{n}_r_onehot")
            s.r_window = sem(f"l{n}_r_window")
            s.r_added = sem(f"l{n}_r_added")
            return s

        L = [edge_sems(0), edge_sems(1)]
        ea_landed, ea_t = sems("ea_landed"), sems("ea_transposed")
        eat_ready, edge_part = sems("eat_ready"), sems("edge_part_summed")
        pre_ready, msg_ready = sems("pre_ready"), sems("msg_ready")
        r_ea_landed, r_ea_t, r_eat_ready = sem("r_ea_landed"), sem("r_ea_transposed"), sem("r_eat_ready")
        r_part, r_pre_ready, r_msg_ready = sem("r_part_summed"), sem("r_pre_ready"), sem("r_msg_ready")

        def node_sems(n):
            s = Names()
            s.stacked = sem(f"n{n}_stacked")
            s.up_done = sem(f"n{n}_up_done")
            s.hid_ready = sem(f"n{n}_hid_ready")
            s.out_done = sem(f"n{n}_out_done")
            s.step = sem(f"n{n}_step")
            s.std_ready = sem(f"n{n}_std_ready")
            s.stored = sem(f"n{n}_stored")
            return s

        N0, N1 = node_sems(0), node_sems(1)
        L[0].nodes, L[1].nodes = N0, N1
        NORM = 7
        x1_t, x1t_ready, acc_set = sem("x1_transposed"), sem("x1t_ready"), sem("acc_set")
        y_summed, y_ready = sem("y_summed"), sem("y_ready")
        W_LOADS = 17

        def tile_at(i, h):
            return i * (SLOTS * GROUP) + h * GROUP

        def short(i, h):
            return isinstance(i, int) and i == iters - 1 and h == 1

        def rows_landed(i, h):
            return 16 * GROUP * (iters - 1) + 16 * last_tiles if short(i, h) else 16 * GROUP * (i + 1)

        def pairs_in_dram(t, c):
            n = pairs - 1 if c == chunks - 1 and t.shape[0] == n_nodes else pairs
            return n * P, t[c * CN:c * CN + n * 2 * P, :].rearrange("(j p q) f -> p j (q f)", p=P, q=2)

        def last_pair(t):
            return t[n_nodes - 2 * last_rows:n_nodes, :].rearrange("(p q) f -> p (q f)", q=2)

        def alone(eng):
            eng.nop(nofuse=True)

        def pair_rows(t, j, n):
            return t[bass.ds(j * 2 * P, n * 2 * P), :].rearrange("(j p q) f -> p j (q f)", p=P, q=2)

        def by_pair(t, n):
            return t[:, 0:n * P].rearrange("p (j e) -> p j e", e=P)

        def branch(eng, flag, when_set, otherwise):
            eng.wait_ge(flag_made, 2)
            with eng.If(eng.value_load(flag[0:1, 0:1], min_val=0, max_val=1)):
                when_set()
            with eng.Else():
                otherwise()

        def edges_and_nodes(eng, group, leftover, stages):
            for h in range(SLOTS):
                group(1, h, False)

            def regular():
                with eng.Fori(2, LAG * STEP // SLOTS) as i:
                    for h in range(SLOTS):
                        group(i, h, False)

                def step(s):
                    j = s - LAG
                    for u in range(STEP):
                        if 2 * u in stages:
                            stages[2 * u](j, s * STEP - 3, 1)
                        group(s * (STEP // SLOTS) + u // SLOTS, u % SLOTS, False)
                        if 2 * u + 1 in stages:
                            stages[2 * u + 1](j, s * STEP - 3, 1)

                with eng.Fori(LAG, STEPS - 1) as s:
                    step(s)
                step(STEPS - 1)
                for u in sorted(stages):
                    stages[u](in_loop, n_groups, REST)

            def other():
                with eng.Fori(2, iters - 1) as i:
                    for h in range(SLOTS):
                        group(i, h, False)
                for h in range(SLOTS):
                    group(iters - 1, h, False)
                branch(eng, has_leftover, leftover, eng.nop)
                if stages:
                    with eng.Fori(0, in_loop) as j:
                        for u in sorted(stages):
                            stages[u](j, n_groups, 1)
                    for u in sorted(stages):
                        stages[u](in_loop, n_groups, REST)

            branch(eng, irregular, other, regular)

        def over_tiles(eng, body):
            with eng.Fori(0, full_tiles) as t:
                body(t, P)
            body(full_tiles, last_edges)

        block = ctx.enter_context(nc.Block())

        @block.sync
        def _(sp):
            whole = full_tiles // P
            rest = full_tiles - whole * P
            sp.wait_ge(pads_set, 3)
            for raw, ap, s in ((src_raw, src, src_landed), (dst_raw, dst, dst_landed)):
                sp.dma_start(raw[:, 0:whole * P].rearrange("p (k e) -> p k e", e=P),
                             ap[0:whole * P * P].rearrange("(k p e) -> p k e", p=P, e=P)).then_inc(s, 16)
                sp.dma_start(raw[0:rest, whole * P:(whole + 1) * P],
                             ap[whole * P * P:full_tiles * P].rearrange("(p e) -> p e", e=P)).then_inc(s, 16)
                sp.dma_start(raw[rest:rest + 1, whole * P:whole * P + last_edges],
                             ap[full_tiles * P:n_edges].rearrange("(p e) -> p e", p=1)).then_inc(s, 16)
            for c in range(chunks):
                cols, part = pairs_in_dram(x, c)
                sp.dma_start(nodes[:, c * CF:c * CF + cols].rearrange("p (j e) -> p j e", e=P), part
                             ).then_inc(x_landed[c], 16)
            sp.dma_start(nodes[0:last_rows, (blocks - 2) * d:], last_pair(x)).then_inc(x_landed[chunks - 1], 16)
            sp.wait_ge(weights_zeroed, 5)
            for diag, w in ((w1_diag, w1), (w2_diag, w2), (wnode_diag, w_msg[0:d, :]),
                            (wedge_diag, w_msg[d:2 * d, :]), (wupd_diag, w_upd)):
                sp.dma_start(diag[0:d, 0:d], w).then_inc(weights_landed, 16)
                sp.dma_start(diag[d:P, d:P], w).then_inc(weights_landed, 16)
            for col, b in ((b1_col, b1), (bupd_col, b_upd)):
                sp.dma_start(col[0:d, :], b.rearrange("(f a) -> f a", a=1)).then_inc(weights_landed, 16)
                sp.dma_start(col[d:P, :], b.rearrange("(f a) -> f a", a=1)).then_inc(weights_landed, 16)
            for many, b in ((b2_rows, b2), (bmsg_rows, b_msg)):
                sp.dma_start(many[:, :], b.rearrange("(a f) -> a f", a=1).to_broadcast([P, d])
                             ).then_inc(weights_landed, 16)
            sp.dma_start(one_eps[:, :], eps.rearrange("(f a) -> f a", a=1).to_broadcast([P, 1])
                         ).then_inc(weights_landed, 16)

            def load_ea(i, h, first):
                n = last_tiles - 1 if short(i, h) else GROUP
                if not first:
                    sp.wait_ge(ea_t[h], i)
                sp.dma_start(ea[:, h, 0:n, :],
                             edge_attr[bass.ds(tile_at(i, h) * P, n * P), :].rearrange("(t p) f -> p t f", p=P)
                             ).then_inc(ea_landed[h], 16)
                if short(i, h):
                    sp.dma_start(ea[0:last_edges, h, n, :], edge_attr[full_tiles * P:n_edges, :]
                                 ).then_inc(ea_landed[h], 16)

            for h in range(SLOTS):
                load_ea(0, h, True)

            def store_y(j, n):
                sp.wait_ge(y_ready, j + 2)
                sp.dma_start(pair_rows(msg_table, j, n), by_pair(y, n)).then_inc(N0.stored, 16)

            with sp.Fori(0, in_loop) as j:
                store_y(j, 1)
            store_y(in_loop, REST)

            def store(j, groups, n):
                sp.wait_ge(N1.step, NORM * j + NORM)
                if n == REST:
                    sp.dma_start(last_pair(out), result[0:last_rows, (n - 1) * P:n * P]).then_inc(N1.stored, 16)
                    n -= 1
                sp.dma_start(pair_rows(out, j, n), by_pair(result, n)).then_inc(N1.stored, 16)

            def leftover():
                def body(t, n):
                    sp.wait_ge(L[1].r_added, t * SWEEPS + 1)
                    sp.dma_start(r_ea[0:n, :], edge_attr[bass.ds(t * P, n), :]).then_inc(r_ea_landed, 16)
                over_tiles(sp, body)

            edges_and_nodes(sp, load_ea, leftover, {3: store})
            sp.wait_ge(N0.stored, 16 * (turns + 1))
            sp.wait_ge(N1.stored, 16 * (turns + 2))

        @block.gpsimd
        def _(pool):
            nc.gpsimd.memset(ident[:, :], 0.0).then_inc(ident_zeroed, 1)
            pool.wait_ge(ident_zeroed, 1)
            nc.gpsimd.affine_select(out=ident[:, :], in_=ident[:, :], compare_op=ALU.not_equal, fill=1.0,
                                    base=0, pattern=[[-1, P]], channel_multiplier=1).then_inc(ident_made, 1)
            nc.gpsimd.iota(iota_i[:, :], pattern=[[1, BANK]], base=0, channel_multiplier=0).then_inc(iota_made, 1)
            nc.gpsimd.iota(taken_i[:, :, :].rearrange("p a b -> p (a b)"), pattern=[[2 * P, STEPS + 1], [0, STEP]],
                           base=2 * P * (1 - LAG), channel_multiplier=0).then_inc(taken_iota, 1)

            def gather_from(table, s, rows_used):
                def body(i, h, first):
                    if not first:
                        pool.wait_ge(rows_used[h], i)
                    pool.wait_ge(s.idx_ready[h], i + 1)
                    alone(pool)
                    for k in range(last_tiles if short(i, h) else GROUP):
                        pool.indirect_dma_start(
                            out=rows[:, h, k * d:(k + 1) * d], out_offset=None, in_=table,
                            in_offset=bass.IndirectOffsetOnAxis(ap=idx_ring[:, h, k:k + 1], axis=0),
                        ).then_inc(s.gathered[h], 16)
                return body

            def leftover_from(table, s):
                def body(t, n):
                    pool.wait_ge(s.r_added, t * SWEEPS + 1)
                    nc.gpsimd.tensor_copy(r_idx[:, :], src_idx[:, bass.ds(t, 1)]).then_inc(s.r_idx, 1)
                    pool.wait_ge(s.r_idx, t + 1)
                    alone(pool)
                    pool.indirect_dma_start(
                        out=r_row[:, :], out_offset=None, in_=table,
                        in_offset=bass.IndirectOffsetOnAxis(ap=r_idx[:, 0:1], axis=0)).then_inc(s.r_gathered, 16)
                return lambda: over_tiles(pool, body)

            def layer(table, s, rows_used):
                group = gather_from(table, s, rows_used)
                for h in range(SLOTS):
                    group(0, h, True)
                edges_and_nodes(pool, group, leftover_from(table, s), {})

            layer(x[:, :], L[0], L[0].windows_done)
            pool.wait_ge(N0.stored, 16 * (turns + 1))
            layer(msg_table[:, :], L[1], pre_ready)

        @block.scalar
        def _(act):
            def copy_src(q):
                nb = min(4, TB - 4 * q)
                act.wait_ge(src_t, q + 1)
                nc.scalar.copy(src_idx[:, 4 * q * P:(4 * q + nb) * P], bank(q)[:, 0:nb * P]).then_inc(src_copied, 1)

            def copy_idx(s, i, h, first):
                if not first:
                    act.wait_ge(s.gathered[h], 16 * GROUP * i)
                nc.scalar.copy(idx_ring[:, h, :], src_idx[:, bass.ds(tile_at(i, h), GROUP)]
                               ).then_inc(s.idx_ready[h], 1)

            copy_src(0)
            act.wait_ge(src_copied, 1)
            for h in range(SLOTS):
                copy_idx(L[0], 0, h, True)
            for q in range(1, 4):
                copy_src(q)

            def nodes_of(j, n, parity):
                return acc[:, bass.ds(j * 2 * P, n * 2 * P)].rearrange("p (n q) -> p n q", q=2)[:, :, parity]

            def pair_half(t, parity):
                return t[parity * d:(parity + 1) * d, :]

            for c in range(chunks):
                act.wait_ge(x_t, c + 1)
                for parity in range(2):
                    last = nc.scalar.copy(nodes_of(c * pairs, pairs, parity), pair_half(x_ps[c % 2][:, 0:CF], parity))
                last.then_inc(acc_started, 1)

            act.wait_ge(src_copied, 4)

            def stack_pair(s, j, groups, n):
                act.wait_ge(s.acc_added, groups)
                for parity in range(2):
                    last = nc.scalar.copy(pair_half(stack[:, 0:n * P], parity), nodes_of(j, n, parity))
                last.then_inc(s.nodes.stacked, 1)

            def hidden(s, func, bias, j, n):
                act.wait_ge(s.up_done, j + 1)
                nc.scalar.activation(hid[:, 0:n * P], wide_ps[:, 0:n * P], func, bias=bias).then_inc(s.hid_ready, 1)

            def root(s, j, n):
                act.wait_ge(s.step, NORM * j + 5)
                nc.scalar.activation(std[:, 0:2 * n], var[:, 0:2 * n], ACT.Sqrt, bias=ln_eps[:, 0:1], scale=1.0 / d
                                     ).then_inc(s.std_ready, 1)

            def hidden0(j, groups, n):
                stack_pair(L[0], j, groups, n)
                hidden(N0, ACT.Relu, b1_col[:, 0:1], j, n)

            def keep_x1(j, groups, n):
                act.wait_ge(x1_t, j + 1)
                nc.scalar.copy(x1t[:, 0:n * P], wide_ps[:, 0:n * P]).then_inc(x1t_ready, 1)
                act.wait_ge(eps_made, 1)
                nc.scalar.copy(nodes[:, bass.ds(j * P, n * P)], x1[:, 0:n * P])
                for parity in range(2):
                    last = nc.scalar.activation(nodes_of(j, n, parity), pair_half(wide_ps[:, 0:n * P], parity), ACT.Copy,
                                                scale=one_eps[parity * d:(parity + 1) * d, 0:1])
                last.then_inc(acc_set, 1)

            edges_and_nodes(act, lambda i, h, first: copy_idx(L[0], i, h, first),
                            lambda: act.wait_ge(L[0].r_added, tiles * SWEEPS + 1),
                            {1: hidden0, 3: lambda j, groups, n: root(N0, j, n), 5: keep_x1})

            def edge(i, h, first):
                if h == 0:
                    copy_idx(L[1], i, 1, first)
                elif not short(i, h):
                    copy_idx(L[1], i + 1, 0, False)
                act.wait_ge(ea_t[h], i + 1)
                if not first:
                    act.wait_ge(edge_part[h], i)
                nc.scalar.copy(eat[:, h, :], eat_ps[h]).then_inc(eat_ready[h], 1)
                act.wait_ge(pre_ready[h], i + 1)
                if not first:
                    act.wait_ge(L[1].windows_done[h], i)
                nc.scalar.activation(msg[:, h, :], pre[:, h, :], ACT.Gelu_apprx_tanh).then_inc(msg_ready[h], 1)

            copy_idx(L[1], 0, 0, True)
            for h in range(SLOTS):
                edge(0, h, True)

            def leftover1():
                def body(t, n):
                    act.wait_ge(r_ea_t, t + 1)
                    nc.scalar.copy(r_eat[:, :], r_eat_ps).then_inc(r_eat_ready, 1)
                    act.wait_ge(r_pre_ready, t + 1)
                    nc.scalar.activation(r_msg[:, :], r_pre[:, :], ACT.Gelu_apprx_tanh).then_inc(r_msg_ready, 1)
                over_tiles(act, body)
                act.wait_ge(L[1].r_added, tiles * SWEEPS + 1)

            def hidden1(j, groups, n):
                stack_pair(L[1], j, groups, n)
                hidden(N1, ACT.Gelu_apprx_tanh, bupd_col[:, 0:1], j, n)

            edges_and_nodes(act, edge, leftover1, {0: hidden1, 1: lambda j, groups, n: root(N1, j, n)})

        @block.vector
        def _(dve):
            last_block = (TB - 1) * P
            nc.vector.memset(src_raw[:, last_block:], 0).then_inc(pads_set, 1)
            nc.vector.memset(dst_raw[:, last_block:], -1).then_inc(pads_set, 1)
            nc.vector.memset(nodes[:, (blocks - 2) * d:], 0.0).then_inc(pads_set, 1)
            for w in (w1_diag, w2_diag, wnode_diag, wedge_diag, wupd_diag):
                nc.vector.memset(w[:, :], 0.0).then_inc(weights_zeroed, 1)
            nc.vector.memset(ln_eps[:, :], LN_EPS)
            nc.vector.memset(acc[:, blocks * P:], 0.0)
            dve.wait_ge(src_landed, 48)
            nc.vector.tensor_copy(src_f[:, :], src_raw[:, :]).then_inc(src_as_f, 1)
            dve.wait_ge(dst_landed, 48)
            nc.vector.tensor_copy(dst_f[:, :], dst_raw[:, :]).then_inc(dst_as_f, 1)
            dve.wait_ge(ident_made, 1)
            nc.vector.tensor_copy(spread[:, :].rearrange("p (g k) -> p g k", k=GROUP),
                                  ident[:, ::GROUP].rearrange("p (g a) -> p g a", a=1)
                                  .to_broadcast([P, P // GROUP, GROUP])).then_inc(spread_made, 1)

            def by_block(t):
                return t.rearrange("p (k e) -> p k e", e=P)

            dve.wait_ge(base_summed, 1)
            nc.vector.tensor_scalar(base_col[:, :], base_ps, 0.0, None, ALU.max).then_inc(base_made, 1)
            dve.wait_ge(base_made, 1)
            dve.wait_ge(src_t, 1)
            dve.wait_ge(dst_as_f, 1)
            dve.wait_ge(src_as_f, 1)
            nc.vector.tensor_tensor(by_block(loc_f), by_block(dst_f[:, :]),
                                    base_col[:, :].rearrange("p (k a) -> p k a", a=1).to_broadcast([P, TB, P]),
                                    ALU.subtract).then_inc(loc_made, 1)
            dve.wait_ge(iota_made, 1)
            nc.vector.tensor_copy(iota_f[:, :], iota_i[:, :])
            dve.wait_ge(taken_iota, 1)
            nc.vector.tensor_scalar(taken[:, :], taken_i[:, :, :].rearrange("p a b -> p (a b)")[:, 3:3 + n_groups],
                                    in_loop * 2 * P, None, ALU.min).then_inc(taken_step, 1)
            dve.wait_ge(taken_step, 1)
            dve.wait_ge(rows_summed, 1)
            nc.vector.tensor_tensor(taken[:, :], taken[:, :], row_ps, ALU.is_gt).then_inc(taken_step, 1)
            nc.vector.tensor_copy(base_row[:, :], row_ps).then_inc(base_row_made, 1)
            dve.wait_ge(taken_step, 2)
            nc.vector.tensor_reduce(late[:, :], taken[:, :], AX.X, ALU.max).then_inc(taken_step, 1)
            for q in range(4):
                nb = min(4, TB - 4 * q)
                dve.wait_ge(loc_t, q + 1)
                nc.vector.tensor_copy(dst_loc[:, 4 * q * P:(4 * q + nb) * P], bank(4 + q)[:, 0:nb * P]
                                      ).then_inc(loc_copied, 1)

            def make_onehot(s, i, h, first):
                if not first:
                    dve.wait_ge(s.windows_done[h], i)
                nc.vector.tensor_tensor(
                    onehot[:, h, :, :],
                    iota_f[:, 0:WINDOW].rearrange("p (a n) -> p a n", a=1).to_broadcast([P, GROUP, WINDOW]),
                    dst_loc[:, bass.ds(tile_at(i, h), GROUP)].rearrange("p (g a) -> p g a", a=1)
                    .to_broadcast([P, GROUP, WINDOW]), ALU.is_equal).then_inc(s.onehot_ready[h], 1)

            def add_window(s, i, h, first):
                g = i * SLOTS + h
                base = dve.value_load(base_row[0:1, bass.ds(g, 1)], min_val=0, max_val=n_nodes - 1)
                dve.wait_ge(s.windows_done[h], i + 1)
                if not (first and h == 0):
                    dve.wait_ge(s.acc_added, g)
                at = acc[:, bass.ds(base, WINDOW)]
                nc.vector.tensor_tensor(at, at, windows[h], ALU.add).then_inc(s.acc_added, 1)

            dve.wait_ge(loc_copied, 4)
            for h in range(SLOTS):
                make_onehot(L[0], 0, h, True)

            nc.vector.tensor_scalar(left_f, loc_f, float(WINDOW), None, ALU.is_ge).then_inc(left_step, 1)
            dve.wait_ge(left_step, 1)
            nc.vector.scalar_tensor_tensor(out=left_f, in0=loc_f, scalar=0.0, in1=left_f,
                                           op0=ALU.is_lt, op1=ALU.add).then_inc(left_step, 1)
            dve.wait_ge(left_step, 2)
            nc.vector.scalar_tensor_tensor(out=left_f, in0=dst_f[:, :], scalar=0.0, in1=left_f,
                                           op0=ALU.is_ge, op1=ALU.mult).then_inc(left_step, 1)
            dve.wait_ge(left_step, 3)
            nc.vector.tensor_reduce(left_max[:, :], left_f, AX.X, ALU.max).then_inc(left_step, 1)
            nc.vector.scalar_tensor_tensor(out=dst_f[:, :], in0=dst_f[:, :], scalar=1.0, in1=left_f,
                                           op0=ALU.add, op1=ALU.mult).then_inc(left_step, 1)
            for s, n in ((L[0].r_added, 1), (L[1].r_added, 1), (y_ready, 1), (N0.stored, 16), (N1.stored, 16)):
                dve.nop().then_inc(s, n)

            dve.wait_ge(base_row_made, 1)
            dve.wait_ge(acc_started, chunks)
            for h in range(SLOTS):
                add_window(L[0], 0, h, True)
            dve.wait_ge(flag_t, 1)
            nc.vector.tensor_reduce(left_one[:, :], flag_ps, AX.X, ALU.max).then_inc(taken_step, 1)
            dve.wait_ge(taken_step, 4)
            nc.vector.tensor_tensor(irregular[:, :], left_one[:, :], late[:, :], ALU.max).then_inc(flag_made, 1)
            nc.vector.tensor_copy(has_leftover[:, :], left_one[:, :]).then_inc(flag_made, 1)
            dve.wait_ge(weights_landed, 16 * W_LOADS)
            nc.vector.tensor_scalar(one_eps[:, :], one_eps[:, :], 1.0, None, ALU.add).then_inc(eps_made, 1)
            dve.wait_ge(x_t, chunks)
            for c in range(chunks):
                part = nodes[:, c * CF:(c + 1) * CF].rearrange("p (b f) -> p b f", f=d)
                nc.vector.tensor_tensor(part, part, b2_rows[:, :].rearrange("p (a f) -> p a f", a=1)
                                        .to_broadcast([P, CHUNK, d]), ALU.add).then_inc(b2_added, 1)

            def edge0(i, h, first):
                make_onehot(L[0], i, h, first)
                add_window(L[0], i, h, first)

            def leftover(s, before):
                def body(t, n):
                    dve.wait_ge(s.r_added, t * SWEEPS + 1)
                    before(t)
                    nc.vector.tensor_scalar(r_key[:, :], dst_left[:, bass.ds(t, 1)], 1.0, None, ALU.subtract
                                            ).then_inc(s.r_key, 1)
                    with dve.Fori(0, SWEEPS) as w:
                        n_done = t * SWEEPS + w
                        dve.wait_ge(s.r_added, n_done + 1)
                        dve.wait_ge(s.r_key, t * (SWEEPS + 1) + w + 1)
                        nc.vector.tensor_scalar(r_onehot[:, :], iota_f[:, :], r_key[:, 0:1], None, ALU.is_equal
                                                ).then_inc(s.r_onehot, 1)
                        dve.wait_ge(s.r_onehot, n_done + 1)
                        nc.vector.tensor_scalar(r_key[:, :], r_key[:, :], float(BANK), None, ALU.subtract
                                                ).then_inc(s.r_key, 1)
                        dve.wait_ge(s.r_window, n_done + 1)
                        at = acc[:, bass.ds(w * BANK, BANK)]
                        nc.vector.tensor_tensor(at, at, r_window_ps, ALU.add).then_inc(s.r_added, 1)
                over_tiles(dve, body)

            def leftover0():
                for q in range(4):
                    nb = min(4, TB - 4 * q)
                    dve.wait_ge(L[0].r_start, q + 1)
                    nc.vector.tensor_copy(dst_left[:, 4 * q * P:(4 * q + nb) * P], bank(6 + q % 2)[:, 0:nb * P]
                                          ).then_inc(L[0].r_left, 1)
                dve.wait_ge(L[0].r_left, 4)
                dve.wait_ge(L[0].acc_added, n_groups)
                leftover(L[0], lambda t: None)

            def blocks_of(t, n):
                return t[:, 0:n * P].rearrange("p (b f) -> p b f", f=d)

            def over_f(t, n):
                return t[:, 0:2 * n].rearrange("p (b a) -> p b a", a=1).to_broadcast([P, 2 * n, d])

            def center(s, j, n):
                dve.wait_ge(s.out_done, j + 1)
                nc.vector.tensor_tensor(v[:, 0:n * P], node_ps[:, 0:n * P], nodes[:, bass.ds(j * P, n * P)], ALU.add
                                        ).then_inc(s.step, 1)
                dve.wait_ge(s.step, NORM * j + 1)
                nc.vector.tensor_reduce(total[:, 0:2 * n], blocks_of(v, n), AX.X, ALU.add).then_inc(s.step, 1)
                dve.wait_ge(s.step, NORM * j + 2)
                nc.vector.scalar_tensor_tensor(out=blocks_of(v, n), in0=over_f(total, n), scalar=-1.0 / d,
                                               in1=blocks_of(v, n), op0=ALU.mult, op1=ALU.add).then_inc(s.step, 1)
                dve.wait_ge(s.step, NORM * j + 3)
                nc.vector.tensor_tensor(sq[:, 0:n * P], v[:, 0:n * P], v[:, 0:n * P], ALU.mult).then_inc(s.step, 1)
                dve.wait_ge(s.step, NORM * j + 4)
                nc.vector.tensor_reduce(var[:, 0:2 * n], blocks_of(sq, n), AX.X, ALU.add).then_inc(s.step, 1)

            def scale(s, j, n, to):
                dve.wait_ge(s.std_ready, j + 1)
                nc.vector.reciprocal(rstd[:, 0:2 * n], std[:, 0:2 * n]).then_inc(s.step, 1)
                dve.wait_ge(s.step, NORM * j + 6)
                nc.vector.tensor_tensor(blocks_of(to, n), blocks_of(v, n), over_f(rstd, n), ALU.mult
                                        ).then_inc(s.step, 1)
                dve.wait_ge(s.step, NORM * j + NORM)

            def norm0(j, groups, n):
                center(N0, j, n)
                scale(N0, j, n, x1)

            def add_bmsg(j, groups, n):
                dve.wait_ge(y_summed, j + 1)
                dve.wait_ge(N0.stored, 16 * (j + 1))
                nc.vector.tensor_tensor(blocks_of(y, n), blocks_of(node_ps, n),
                                        bmsg_rows[:, :].rearrange("p (a f) -> p a f", a=1)
                                        .to_broadcast([P, 2 * n, d]), ALU.add).then_inc(y_ready, 1)

            def norm1(j, groups, n):
                dve.wait_ge(N1.stored, 16 * (j + 1))
                scale(N1, j, n, result)

            dve.wait_ge(b2_added, chunks)
            edges_and_nodes(dve, edge0, leftover0, {2: norm0, 5: add_bmsg})

            def edge1(i, h, first):
                make_onehot(L[1], i, h, first)
                dve.wait_ge(edge_part[h], i + 1)
                dve.wait_ge(L[1].gathered[h], rows_landed(i, h))
                if not first:
                    dve.wait_ge(msg_ready[h], i)
                nc.vector.tensor_tensor(pre[:, h, :], msg_ps[h], rows[:, h, :], ALU.add).then_inc(pre_ready[h], 1)
                add_window(L[1], i, h, first)

            dve.wait_ge(acc_set, turns)
            for h in range(SLOTS):
                edge1(0, h, True)

            def before1(t):
                dve.wait_ge(r_part, t + 1)
                dve.wait_ge(L[1].r_gathered, 16 * (t + 1))
                nc.vector.tensor_tensor(r_pre[:, :], r_pre_ps, r_row[:, :], ALU.add).then_inc(r_pre_ready, 1)

            def leftover1():
                dve.wait_ge(L[1].acc_added, n_groups)
                leftover(L[1], before1)

            edges_and_nodes(dve, edge1, leftover1, {0: lambda j, groups, n: center(N1, j, n), 1: norm1})

        @block.tensor
        def _(pe):
            def block_t(out_bank, q, source, signal):
                nb = min(4, TB - 4 * q)
                for k in range(nb):
                    last = nc.tensor.transpose(out_bank[:, k * P:(k + 1) * P],
                                               source[:, (4 * q + k) * P:(4 * q + k + 1) * P], ident[:, :])
                last.then_inc(signal, 1)

            pe.wait_ge(ident_made, 1)
            pe.wait_ge(src_as_f, 1)
            for q in range(4):
                block_t(bank(q), q, src_f, src_t)
            pe.wait_ge(dst_as_f, 1)
            pe.wait_ge(spread_made, 1)
            nc.tensor.matmul(base_ps, spread[:, :], dst_f[:, ::P], start=True, stop=True).then_inc(base_summed, 1)
            pe.wait_ge(base_made, 1)
            for k in range(TB):
                last = nc.tensor.matmul(row_ps[:, k * P // GROUP:(k + 1) * P // GROUP], base_col[:, k:k + 1],
                                        ident[:, ::GROUP], start=True, stop=True)
            last.then_inc(rows_summed, 1)
            pe.wait_ge(loc_made, 1)
            for q in range(4):
                if q == 3:
                    pe.wait_ge(base_row_made, 1)
                block_t(bank(4 + q), q, loc_f, loc_t)

            def sum_group(s, rhs, i, h, first):
                pe.wait_ge(s.onehot_ready[h], i + 1)
                if not first:
                    pe.wait_ge(s.acc_added, (i - 1) * SLOTS + h + 1)
                n = last_tiles if short(i, h) else GROUP
                for k in range(n):
                    last = nc.tensor.matmul(windows[h], rhs[:, h, k * d:(k + 1) * d], onehot[:, h, k, :],
                                            start=k == 0, stop=k == n - 1)
                last.then_inc(s.windows_done[h], 1)

            def edge0(i, h, first):
                pe.wait_ge(L[0].gathered[h], rows_landed(i, h))
                sum_group(L[0], rows, i, h, first)

            pe.wait_ge(loc_copied, 4)
            for c in range(chunks):
                pe.wait_ge(x_landed[c], 32 if c == chunks - 1 else 16)
                if c >= 2:
                    pe.wait_ge(acc_started, c - 1)
                for j in range(pairs):
                    last = nc.tensor.transpose(x_ps[c % 2][:, j * P:(j + 1) * P],
                                               nodes[:, c * CF + j * P:c * CF + (j + 1) * P], ident[:, :])
                last.then_inc(x_t, 1)
                if c == 4:
                    pe.wait_ge(src_copied, 4)
                    edge0(0, 0, True)
            edge0(0, 1, True)
            pe.wait_ge(acc_started, chunks)
            pe.wait_ge(left_step, 4)
            nc.tensor.transpose(flag_ps, left_max[:, 0:1], ident[:, :]).then_inc(flag_t, 1)

            def sweeps(s, t, rhs):
                alone(pe)
                with pe.Fori(0, SWEEPS) as w:
                    pe.wait_ge(s.r_onehot, t * SWEEPS + w + 1)
                    nc.tensor.matmul(r_window_ps, rhs[:, :], r_onehot[:, :], start=True, stop=True
                                     ).then_inc(s.r_window, 1)

            def leftover0():
                pe.wait_ge(flag_made, 2)
                pe.wait_ge(left_step, 5)
                for q in range(4):
                    if q >= 2:
                        pe.wait_ge(L[0].r_left, q - 1)
                    block_t(bank(6 + q % 2), q, dst_f, L[0].r_start)
                pe.wait_ge(L[0].r_left, 4)

                def body(t, n):
                    pe.wait_ge(L[0].r_gathered, 16 * (t + 1))
                    sweeps(L[0], t, r_row)
                over_tiles(pe, body)

            def up(s, w, j, n):
                pe.wait_ge(s.stacked, j + 1)
                nc.tensor.matmul(wide_ps[:, 0:n * P], w[:, :], stack[:, 0:n * P], start=True, stop=True
                                 ).then_inc(s.up_done, 1)

            def from_pairs(t, w, n, signal):
                for k in range(n):
                    last = nc.tensor.matmul(node_ps[:, k * P:(k + 1) * P], t[:, k * P:(k + 1) * P], w[:, :],
                                            start=True, stop=True)
                last.then_inc(signal, 1)

            def pairs_t(to, t, n, signal):
                alone(pe)
                for k in range(n):
                    last = nc.tensor.transpose(to[:, k * P:(k + 1) * P], t[:, k * P:(k + 1) * P], ident[:, :])
                last.then_inc(signal, 1)

            def up0(j, groups, n):
                up(N0, w1_diag, j, n)

            def out0(j, groups, n):
                pe.wait_ge(N0.hid_ready, j + 1)
                pe.wait_ge(y_ready, j + 1)
                from_pairs(hid, w2_diag, n, N0.out_done)

            def message_rows(j, groups, n):
                pe.wait_ge(N0.step, NORM * j + NORM)
                pairs_t(wide_ps, x1, n, x1_t)
                pe.wait_ge(x1t_ready, j + 1)
                from_pairs(x1t, wnode_diag, n, y_summed)

            def node_products1(j, groups, n):
                up(N1, wupd_diag, j, n)
                pe.wait_ge(N1.hid_ready, j + 1)
                pairs_t(node_ps, hid, n, N1.out_done)

            pe.wait_ge(weights_landed, 16 * W_LOADS)
            edges_and_nodes(pe, edge0, leftover0, {0: up0, 1: out0, 4: message_rows})

            def edge1(i, h, first):
                pe.wait_ge(ea_landed[h], 16 * (i + 1) + (16 if short(i, h) else 0))
                if not first:
                    pe.wait_ge(eat_ready[h], i)
                alone(pe)
                for k in range(GROUP // 2):
                    last = nc.tensor.transpose(eat_ps[h][:, k * P:(k + 1) * P],
                                               ea[:, h, 2 * k:2 * k + 2, :].rearrange("p a f -> p (a f)"), ident[:, :])
                last.then_inc(ea_t[h], 1)
                pe.wait_ge(eat_ready[h], i + 1)
                if not first:
                    pe.wait_ge(pre_ready[h], i)
                for k in range(GROUP // 2):
                    last = nc.tensor.matmul(msg_ps[h][:, k * P:(k + 1) * P], eat[:, h, k * P:(k + 1) * P],
                                            wedge_diag[:, :], start=True, stop=True)
                last.then_inc(edge_part[h], 1)
                pe.wait_ge(msg_ready[h], i + 1)
                sum_group(L[1], msg, i, h, first)

            for h in range(SLOTS):
                edge1(0, h, True)

            def leftover1():
                def body(t, n):
                    pe.wait_ge(r_ea_landed, 16 * (t + 1))
                    alone(pe)
                    nc.tensor.transpose(r_eat_ps, r_ea[:, :], ident[:, :]).then_inc(r_ea_t, 1)
                    pe.wait_ge(r_eat_ready, t + 1)
                    nc.tensor.matmul(r_pre_ps, r_eat[:, :], wedge_diag[0:d, 0:d], start=True, stop=True
                                     ).then_inc(r_part, 1)
                    pe.wait_ge(r_msg_ready, t + 1)
                    sweeps(L[1], t, r_msg)
                over_tiles(pe, body)

            edges_and_nodes(pe, edge1, leftover1, {0: node_products1})


_INS = ["x", "src", "dst", "edge_attr_64", "L0_gnn_W1", "L0_gnn_b1", "L0_gnn_W2", "L0_gnn_b2",
        "L1_gnn_W_msg", "L1_gnn_b_msg", "L1_gnn_W_upd", "L1_gnn_b_upd", "L1_gnn_eps"]


def kernel(**inputs):
    import numpy as _np
    import concourse.bacc as _bacc
    from concourse import mybir as _mybir
    from concourse.bass_utils import run_bass_kernel_spmd as _run

    nc = _bacc.Bacc("TRN2", target_bir_lowering=False, num_devices=1)
    arrays, args = {}, []
    for name in _INS:
        a = _np.ascontiguousarray(inputs[name])
        arrays[f"in_{name}"] = a
        args.append(nc.dram_tensor(f"in_{name}", a.shape, _mybir.dt.from_np(a.dtype), kind="ExternalInput").ap())
    shape = inputs["x"].shape
    args.append(nc.dram_tensor("out_0", shape, F32, kind="ExternalOutput").ap())
    gnn_kernel(nc, *args)
    r = _run(nc, [arrays], core_ids=[0])
    return r.results[0]["out_0"]
```
